# Optimizing a Trainium2 kernel written in Bass

```python
import numpy as np
import jax
import jax.numpy as jnp

def _softmax(x, axis=-1):
    return jax.nn.softmax(x, axis=axis)

def _gelu(x):
    return jax.nn.gelu(x, approximate=True)

def _silu(x):
    return jax.nn.silu(x)

def _sigmoid(x):
    return jax.nn.sigmoid(x)

def _layernorm(x, axis=-1, eps=1e-05):
    m = jnp.mean(x, axis=axis, keepdims=True)
    v = jnp.var(x, axis=axis, keepdims=True)
    return (x - m) / jnp.sqrt(v + eps)

def _scatter_add(tgt, idx, src, axis=0):
    return tgt.at[idx].add(src)

def _segment_sum(src, seg, n):
    return jax.ops.segment_sum(src, seg, n)
kernel_name = 'mk_seq_postln_d1_jaxref_r4_f0510f'

def setup_inputs(seed: int=0):
    np.random.seed(seed)
    _w = jnp.asarray

    def _L0_attn_setup():
        import jax, jax.numpy as jnp
        import numpy as np
        DIM = 256
        D_STATE = 16
        EXPAND = 2
        D_CONV = 4
        D_INNER = DIM * EXPAND
        DT_RANK = (DIM + 15) // 16
        BATCH = 2
        SEQ = 256

        def _selective_scan(u, delta, A, B, C, D):
            dA = jnp.exp(jnp.einsum('bld,dn->lbdn', delta, A))
            dBu = jnp.einsum('bld,bln,bdl->lbdn', delta, B, u)
            Ct = jnp.transpose(C, (1, 0, 2))

            def step(carry, inp):
                a, bu, c = inp
                carry = a * carry + bu
                y = jnp.einsum('bdn,bn->bd', carry, c)
                return (carry, y)
            x0 = jnp.zeros(dA.shape[1:], dA.dtype)
            _, ys = jax.lax.scan(step, x0, (dA, dBu, Ct))
            y = jnp.transpose(ys, (1, 2, 0))
            return y + u * D[:, None]
        key = jax.random.key(seed)
        ks = jax.random.split(key, 8)
        s = 0.02
        A = jnp.broadcast_to(jnp.arange(1, D_STATE + 1, dtype=jnp.float32), (D_INNER, D_STATE))
        return {'x': jax.random.normal(ks[0], (BATCH, SEQ, DIM), jnp.float32), 'in_w': jax.random.normal(ks[1], (2 * D_INNER, DIM), jnp.float32) * s, 'conv_w': jax.random.normal(ks[2], (D_INNER, 1, D_CONV), jnp.float32) * s, 'conv_b': jnp.zeros((D_INNER,), jnp.float32), 'xproj_w': jax.random.normal(ks[3], (DT_RANK + 2 * D_STATE, D_INNER), jnp.float32) * s, 'dt_w': jax.random.normal(ks[4], (D_INNER, DT_RANK), jnp.float32) * s, 'dt_b': jax.random.normal(ks[5], (D_INNER,), jnp.float32) * s, 'A_log': jnp.log(A), 'D': jnp.ones((D_INNER,), jnp.float32), 'out_w': jax.random.normal(ks[6], (DIM, D_INNER), jnp.float32) * s}
    _L0_attn_in = _L0_attn_setup()

    def _L0_ffn_setup():
        import jax, jax.numpy as jnp
        import numpy as np
        D_IN, D_HID = (256, 1024)

        def _ternary(key, shape):
            return jax.random.randint(key, shape, -1, 2).astype(jnp.float32)

        def _tlin(x, w, s):
            return jnp.einsum('bsi,oi->bso', x, w) * s
        key = jax.random.key(seed)
        ks = jax.random.split(key, 12)
        inv = lambda fan: 1.0 / np.sqrt(fan).astype(np.float32)
        return {'x': jax.random.normal(ks[0], (4, 512, D_IN), dtype=jnp.float32), 'w1_w': _ternary(ks[1], (D_HID, D_IN)), 'w1_s': jax.random.uniform(ks[2], (D_HID,), dtype=jnp.float32) * inv(D_IN), 'w2_w': _ternary(ks[3], (D_HID, D_IN)), 'w2_s': jax.random.uniform(ks[4], (D_HID,), dtype=jnp.float32) * inv(D_IN), 'h1_w': _ternary(ks[5], (D_HID, D_HID)), 'h1_s': jax.random.uniform(ks[6], (D_HID,), dtype=jnp.float32) * inv(D_HID), 'h2_w': _ternary(ks[7], (D_HID, D_HID)), 'h2_s': jax.random.uniform(ks[8], (D_HID,), dtype=jnp.float32) * inv(D_HID), 'w3_w': _ternary(ks[9], (D_IN, D_HID)), 'w3_s': jax.random.uniform(ks[10], (D_IN,), dtype=jnp.float32) * inv(D_HID)}
    _L0_ffn_in = _L0_ffn_setup()
    _d = {'L0_attn_x': _L0_attn_in['x'], 'L0_attn_in_w': _L0_attn_in['in_w'], 'L0_attn_conv_w': _L0_attn_in['conv_w'], 'L0_attn_conv_b': _L0_attn_in['conv_b'], 'L0_attn_xproj_w': _L0_attn_in['xproj_w'], 'L0_attn_dt_w': _L0_attn_in['dt_w'], 'L0_attn_dt_b': _L0_attn_in['dt_b'], 'L0_attn_A_log': _L0_attn_in['A_log'], 'L0_attn_D': _L0_attn_in['D'], 'L0_attn_out_w': _L0_attn_in['out_w'], 'L0_ffn_w1_w': _L0_ffn_in['w1_w'], 'L0_ffn_w1_s': _L0_ffn_in['w1_s'], 'L0_ffn_w2_w': _L0_ffn_in['w2_w'], 'L0_ffn_w2_s': _L0_ffn_in['w2_s'], 'L0_ffn_h1_w': _L0_ffn_in['h1_w'], 'L0_ffn_h1_s': _L0_ffn_in['h1_s'], 'L0_ffn_h2_w': _L0_ffn_in['h2_w'], 'L0_ffn_h2_s': _L0_ffn_in['h2_s'], 'L0_ffn_w3_w': _L0_ffn_in['w3_w'], 'L0_ffn_w3_s': _L0_ffn_in['w3_s']}
    _x0 = _d['L0_attn_x']
    _d['L0_attn_x'] = jax.random.normal(jax.random.fold_in(jax.random.key(seed), 1), (16, 512, 256), dtype=_x0.dtype)
    del _x0
    return _d

def reference(L0_attn_x, L0_attn_in_w, L0_attn_conv_w, L0_attn_conv_b, L0_attn_xproj_w, L0_attn_dt_w, L0_attn_dt_b, L0_attn_A_log, L0_attn_D, L0_attn_out_w, L0_ffn_w1_w, L0_ffn_w1_s, L0_ffn_w2_w, L0_ffn_w2_s, L0_ffn_h1_w, L0_ffn_h1_s, L0_ffn_h2_w, L0_ffn_h2_s, L0_ffn_w3_w, L0_ffn_w3_s):

    def _L0_attn_ref(x, in_w, conv_w, conv_b, xproj_w, dt_w, dt_b, A_log, D, out_w):
        import jax, jax.numpy as jnp
        import numpy as np
        DIM = 256
        D_STATE = 16
        EXPAND = 2
        D_CONV = 4
        D_INNER = DIM * EXPAND
        DT_RANK = (DIM + 15) // 16
        BATCH = 2
        SEQ = 256

        def _selective_scan(u, delta, A, B, C, D):
            dA = jnp.exp(jnp.einsum('bld,dn->lbdn', delta, A))
            dBu = jnp.einsum('bld,bln,bdl->lbdn', delta, B, u)
            Ct = jnp.transpose(C, (1, 0, 2))

            def step(carry, inp):
                a, bu, c = inp
                carry = a * carry + bu
                y = jnp.einsum('bdn,bn->bd', carry, c)
                return (carry, y)
            x0 = jnp.zeros(dA.shape[1:], dA.dtype)
            _, ys = jax.lax.scan(step, x0, (dA, dBu, Ct))
            y = jnp.transpose(ys, (1, 2, 0))
            return y + u * D[:, None]
        b, l, d = x.shape
        xr = x @ in_w.T
        xx, res = jnp.split(xr, 2, axis=-1)
        xx = jnp.transpose(xx, (0, 2, 1))
        xx = jax.lax.conv_general_dilated(xx, conv_w, window_strides=(1,), padding=[(D_CONV - 1, 0)], dimension_numbers=('NCH', 'OIH', 'NCH'), feature_group_count=D_INNER) + conv_b[None, :, None]
        xx = jax.nn.silu(xx)
        A = -jnp.exp(A_log)
        x_dbl = jnp.einsum('bdl,kd->blk', xx, xproj_w)
        delta, B, C = jnp.split(x_dbl, [DT_RANK, DT_RANK + D_STATE], axis=-1)
        delta = jax.nn.softplus(delta @ dt_w.T + dt_b)
        y = _selective_scan(xx, delta, A, B, C, D)
        y = y * jax.nn.silu(jnp.transpose(res, (0, 2, 1)))
        return jnp.transpose(y, (0, 2, 1)) @ out_w.T

    def _L0_ffn_ref(x, w1_w, w1_s, w2_w, w2_s, h1_w, h1_s, h2_w, h2_s, w3_w, w3_s):
        import jax, jax.numpy as jnp
        import numpy as np
        D_IN, D_HID = (256, 1024)

        def _ternary(key, shape):
            return jax.random.randint(key, shape, -1, 2).astype(jnp.float32)

        def _tlin(x, w, s):
            return jnp.einsum('bsi,oi->bso', x, w) * s
        h = jax.nn.silu(_tlin(x, w1_w, w1_s)) * _tlin(x, w2_w, w2_s)
        h = jax.nn.gelu(_tlin(h, h1_w, h1_s), approximate=False)
        h = jax.nn.gelu(_tlin(h, h2_w, h2_s), approximate=False)
        return _tlin(h, w3_w, w3_s)
    x = L0_attn_x
    x = _layernorm(x + _L0_attn_ref(x, L0_attn_in_w, L0_attn_conv_w, L0_attn_conv_b, L0_attn_xproj_w, L0_attn_dt_w, L0_attn_dt_b, L0_attn_A_log, L0_attn_D, L0_attn_out_w), axis=-1)
    x = _layernorm(x + _L0_ffn_ref(x, L0_ffn_w1_w, L0_ffn_w1_s, L0_ffn_w2_w, L0_ffn_w2_s, L0_ffn_h1_w, L0_ffn_h1_s, L0_ffn_h2_w, L0_ffn_h2_s, L0_ffn_w3_w, L0_ffn_w3_s), axis=-1)
    return x

_drawn_inputs = setup_inputs


def setup_inputs(seed=0):
    import zlib

    import numpy as np

    out = dict(_drawn_inputs(seed))
    spreads = {'L0_attn_conv_b': (0.0, 0.8), 'L0_attn_D': (1.0, 0.6)}
    factors = {'L0_attn_in_w': 8.0,
     'L0_attn_conv_w': 8.0,
     'L0_attn_xproj_w': 8.0,
     'L0_attn_dt_w': 8.0,
     'L0_attn_dt_b': 8.0,
     'L0_attn_A_log': 8.0,
     'L0_attn_out_w': 8.0,
     'L0_ffn_w1_w': 8.0,
     'L0_ffn_w1_s': 8.0,
     'L0_ffn_w2_w': 8.0,
     'L0_ffn_w2_s': 8.0,
     'L0_ffn_h1_w': 8.0,
     'L0_ffn_h1_s': 8.0,
     'L0_ffn_h2_w': 8.0,
     'L0_ffn_h2_s': 8.0,
     'L0_ffn_w3_w': 8.0,
     'L0_ffn_w3_s': 8.0}
    for name, (base, spread) in spreads.items():
        noise = np.random.default_rng([zlib.crc32(name.encode()), seed]).standard_normal(out[name].shape)
        drawn = base * np.exp(spread * noise) if base else spread * noise
        out[name] = jnp.asarray(drawn.astype(out[name].dtype))
    for name, factor in factors.items():
        out[name] = (out[name] * factor).astype(out[name].dtype)
    return out
```

```python
from contextlib import ExitStack

import concourse.bass as bass
from concourse import mybir

F32 = mybir.dt.float32
F32R = mybir.dt.float32r
I32 = mybir.dt.int32
ALU = mybir.AluOpType
ACT = mybir.ActivationFunctionType

P = 128
BATCH, SEQ, DIM = 16, 512, 256
INNER, STATES, RANK, TAPS, HIDDEN = 512, 16, 16, 4, 1024
KD = DIM // P
DC = INNER // P
HC = HIDDEN // P
TT = SEQ // P
TILES = STATES * DC
DBL = RANK + 2 * STATES
EPS = 1e-5

C_CONV, C_CONVB, C_D, C_DTB, C_ALOG = 0, TAPS, TAPS + 1, TAPS + 2, TAPS + 3
CHAN = TAPS + 3 + STATES

L1_SLOTS, W3_SLOTS = HC // 2, 2
SLOTS = L1_SLOTS + 2 * HC + W3_SLOTS
SLOT_COLS = HC * P
RING = 4

BANKS = 4
J_XT, J_XX, J_DBL, J_RES, J_DT = 0, 2, 6, 7, 11
J_TILE = 15
J_OUT = J_TILE + TILES
J_X1T = J_OUT + 2
ATTN_JOBS = J_X1T + KD
FRONT_JOBS = J_TILE
TAIL_JOBS = 2 + KD

BC_RING = 4
WORK = 6
LEAD = 3
X32 = 4

GELU_PHASE = 4
GELU_AT = [32, 40, 50, 58]
L1_AT = 3


def build(nc, x, in_wT, chan, xproj_wT, dt_wT, out_wT, ffn_w, ffn_s, w3_s, ident_in, out):
    bc_dram = nc.dram_tensor("bc_rows", [BATCH, 2 * STATES, SEQ], F32, kind="Internal").ap()
    w_dram = nc.dram_tensor("split_weights", [2, SLOTS, P, SLOT_COLS], F32, kind="Internal").ap()

    with ExitStack() as ctx:
        def sb(name, shape, dt=F32):
            return ctx.enter_context(nc.sbuf_tensor(name, shape, dt))

        def sem(name):
            return ctx.enter_context(nc.semaphore(name))

        ident = sb("ident", [P, P])
        inw = sb("inw", [P, KD, 2 * INNER])
        outw = sb("outw", [P, DC, DIM])
        xprojw = sb("xprojw", [P, DC, DBL])
        dtw = sb("dtw", [RANK, INNER])
        ch = sb("ch", [P, DC, CHAN])
        fs = sb("fs", [P, 4, HC])
        w3s = sb("w3s", [P, DIM])
        conv_half = sb("conv_half", [P, DC, TAPS + 1])
        a_neg = sb("a_neg", [P, DC, STATES])
        s1_half = sb("s1_half", [P, HC])
        s12_half = sb("s12_half", [P, HC])
        minus_half = sb("minus_half", [P, TT])
        eps = sb("eps", [P, TT])
        ones = sb("ones", [P, 1])
        low_sums = sb("low_sums", [P, SLOTS])
        low_sum = sb("low_sum", [P, 1])
        low_flag = sb("low_flag", [1, 1])
        xt = sb("xt", [P, TT, DIM])
        xT = sb("xT", [P, KD, SEQ])
        u = sb("u", [P, DC, SEQ])
        v = sb("v", [P, DC, SEQ])
        delta = sb("delta", [P, DC, SEQ])
        y = sb("y", [P, DC, SEQ])
        xdbl = sb("xdbl", [DBL, SEQ])
        bc = sb("bc", [P, BC_RING, 2, SEQ])
        work = sb("work", [P, WORK, SEQ])
        ring = sb("ring", [P, RING, SLOT_COLS], F32R)
        x1 = sb("x1", [P, TT, DIM])
        x1T_hi = sb("x1T_hi", [P, KD, SEQ], F32R)
        x1T_lo = sb("x1T_lo", [P, KD, SEQ], F32R)
        ha_hi = sb("ha_hi", [P, HC, SEQ], F32R)
        ha_lo = sb("ha_lo", [P, HC, SEQ], F32R)
        hb_hi = sb("hb_hi", [P, HC, SEQ], F32R)
        hb_lo = sb("hb_lo", [P, HC, SEQ], F32R)
        gate = sb("gate", [P, 2, SEQ])
        x32 = sb("x32", [P, X32, SEQ])
        out_st = sb("out_st", [P, TT, DIM])
        stats = sb("stats", [P, TT, 6])
        stats_seen = sb("stats_seen", [P, 1])
        mv = sb("mv", [P, TT, 2])
        var_eps = sb("var_eps", [P, TT])
        rstd = sb("rstd", [P, TT])

        raw = work[:, 0:4, :].rearrange("p (s a) l -> p s (a l)", s=2)
        split_hi = ha_hi[:, 0:4, :].rearrange("p (s a) l -> p s (a l)", s=2)
        split_lo = ha_lo[:, 0:4, :].rearrange("p (s a) l -> p s (a l)", s=2)
        sp_w = work[:, 0:DC, :]

        apsum = [ctx.enter_context(nc.psum_tensor(f"apsum{i}", [P, SEQ], F32)) for i in range(BANKS)]
        fpsum = [ctx.enter_context(nc.psum_tensor(f"fpsum{i}", [P, SEQ], F32)) for i in range(BANKS)]

        const_loaded = sem("const_loaded")
        raw_loaded = [sem(f"raw_loaded{i}") for i in range(2)]
        split_stored = [sem(f"split_stored{i}") for i in range(2)]
        x_loaded = sem("x_loaded")
        bc_stored = sem("bc_stored")
        bc_loaded = [sem(f"bc_loaded{i}") for i in range(BC_RING)]
        ring_loaded = [sem(f"ring_loaded{i}") for i in range(RING)]
        out_stored = sem("out_stored")
        const_dve = sem("const_dve")
        const_exp = sem("const_exp")
        const_pool = sem("const_pool")
        split_hi_done = sem("split_hi_done")
        split_lo_done = sem("split_lo_done")
        split_sum_done = sem("split_sum_done")
        low_summed = sem("low_summed")
        low_total = sem("low_total")
        flag_ready = sem("flag_ready")
        pe_front = sem("pe_front")
        pe_tail = sem("pe_tail")
        pe_l1 = sem("pe_l1")
        pe_hid = sem("pe_hid")
        pe_w3 = sem("pe_w3")
        xT_ready = sem("xT_ready")
        conv_base = sem("conv_base")
        conv_taps = sem("conv_taps")
        u_tanh = sem("u_tanh")
        u_ready = sem("u_ready")
        v_tanh = sem("v_tanh")
        v_ready = sem("v_ready")
        xdbl_ready = sem("xdbl_ready")
        dt_ready = sem("dt_ready")
        act_softplus = sem("act_softplus")
        dve_softplus = sem("dve_softplus")
        y_init = sem("y_init")
        du_ready = sem("du_ready")
        dA_ready = sem("dA_ready")
        dBu_ready = sem("dBu_ready")
        scan_done = sem("scan_done")
        hC_done = sem("hC_done")
        y_added = sem("y_added")
        y_gated = sem("y_gated")
        z_ready = sem("z_ready")
        ln_stats = sem("ln_stats")
        ln_aggr = sem("ln_aggr")
        ln_eps = sem("ln_eps")
        ln_rstd = sem("ln_rstd")
        x1_ready = sem("x1_ready")
        x1_hi = sem("x1_hi")
        x1_lo = sem("x1_lo")
        l1_tanh = sem("l1_tanh")
        l1_gate = sem("l1_gate")
        l1_x32 = sem("l1_x32")
        gelu_x32 = sem("gelu_x32")
        ffn_hi = sem("ffn_hi")
        ffn_lo = sem("ffn_lo")
        w3_scaled = sem("w3_scaled")
        z2_ready = sem("z2_ready")
        out_ready = sem("out_ready")

        block = ctx.enter_context(nc.Block())

        CONST_LOADS, CONST_DVE = 8, 7

        def wait_attn_bank(eng, job, b):
            if job < BANKS:
                prev, row = {0: J_OUT + 1, 1: J_X1T, 2: J_X1T + 1, 3: J_OUT}[job], b - 1
            else:
                prev, row = job - BANKS, b
            if isinstance(row, int) and row < 0:
                return
            if prev < J_XX:
                eng.wait_ge(xT_ready, row * KD + (prev + 1))
            elif prev < J_DBL:
                eng.wait_ge(conv_taps, row * (DC * (TAPS - 1)) + (DC * (TAPS - 2) + prev - J_XX + 1))
            elif prev < J_RES:
                eng.wait_ge(xdbl_ready, row + 1)
            elif prev < J_DT:
                eng.wait_ge(v_ready, row * DC + (prev - J_RES + 1))
            elif prev < J_TILE:
                eng.wait_ge(dt_ready, row * DC + (prev - J_DT + 1))
            elif prev < J_OUT:
                eng.wait_ge(hC_done, row * TILES + (prev - J_TILE + 1))
            elif prev < J_X1T:
                eng.wait_ge(z_ready, row * 2 + (prev - J_OUT + 1))
            else:
                eng.wait_ge(x1_lo, row * KD + (prev - J_X1T + 1))

        @block.sync
        def _(sp):
            sp.sem_inc(out_stored, 16)
            for dst, src in ((ident[:], ident_in), (inw[:], in_wT), (ch[:], chan), (xprojw[:], xproj_wT),
                             (dtw[:], dt_wT), (outw[:], out_wT), (fs[:], ffn_s),
                             (w3s[:], w3_s.partition_broadcast(P))):
                sp.dma_start(dst, src).then_inc(const_loaded, 16)
            sp.dma_start(xt[:], x[0]).then_inc(x_loaded, 16)

            for s in range(2):
                sp.dma_start(raw[:, s, :], ffn_w[s]).then_inc(raw_loaded[s], 16)
            def store_parts(i, s):
                sp.wait_ge(split_lo_done, 2 * i + (s + 1))
                sp.dma_start(w_dram[0, 2 * i + s], split_hi[:, s, :].bitcast(F32)).then_inc(split_stored[s], 16)
                sp.dma_start(w_dram[1, 2 * i + s], split_lo[:, s, :].bitcast(F32)).then_inc(split_stored[s], 16)

            with sp.Fori(0, SLOTS // 2 - 1) as i:
                for s in range(2):
                    store_parts(i, s)
                    sp.wait_ge(split_sum_done, 2 * i + (s + 1))
                    sp.dma_start(raw[:, s, :], ffn_w[2 * i + (s + 2)]).then_inc(raw_loaded[s], 16)
            for s in range(2):
                store_parts(SLOTS // 2 - 1, s)
            for s in range(2):
                sp.wait_ge(split_stored[s], 16 * SLOTS)
            sp.wait_ge(flag_ready, 1)
            general = sp.value_load(low_flag[0:1, 0:1].bitcast(I32))

            def store_bc(b):
                sp.wait_ge(xdbl_ready, b + 1)
                sp.dma_start(bc_dram[b], xdbl[RANK:DBL, :]).then_inc(bc_stored, 16)

            def load_weights(f, entries, parts):
                for e in entries:
                    if e >= RING:
                        slot = (e - RING) // parts
                        if slot < L1_SLOTS:
                            sp.wait_ge(pe_l1, f * 2 * HC + 4 * (slot + 1))
                        elif slot < L1_SLOTS + 2 * HC:
                            sp.wait_ge(pe_hid, f * 2 * HC + (slot - L1_SLOTS + 1))
                        else:
                            sp.wait_ge(pe_w3, f * 2 + 2)
                    sp.dma_start(ring[:, e % RING, :].bitcast(F32),
                                 w_dram[e % parts, e // parts]).then_inc(ring_loaded[e % RING], 16)

            def store_out(f):
                sp.wait_ge(out_ready, f * TT + TT)
                sp.dma_start(out[f], out_st[:]).then_inc(out_stored, 16)

            def program(parts):
                with sp.Fori(1, BATCH) as b:
                    sp.wait_ge(x1_ready, b * TT)
                    sp.dma_start(xt[:], x[b]).then_inc(x_loaded, 16)
                    load_weights(b - 1, range(RING), parts)
                    store_bc(b)
                    load_weights(b - 1, range(RING, SLOTS * parts), parts)
                    store_out(b - 1)
                sp.wait_ge(x1_ready, BATCH * TT)
                load_weights(BATCH - 1, range(SLOTS * parts), parts)
                store_out(BATCH - 1)

            store_bc(0)
            with sp.If(general > 0):
                program(2)
            with sp.Else():
                program(1)
            sp.wait_ge(out_stored, 16 * BATCH + 16)
            sp.wait_ge(bc_stored, 16 * BATCH)

        @block.tensor
        def _(pe):
            pe.wait_ge(const_loaded, 16 * CONST_LOADS)
            pe.wait_ge(const_dve, CONST_DVE)
            pe.wait_ge(low_summed, 1)
            nc.tensor.matmul(fpsum[0][0:1, 0:1], low_sum[:], ones[:], start=True, stop=True).then_inc(low_total, 1)
            pe.wait_ge(flag_ready, 1)
            general = pe.value_load(low_flag[0:1, 0:1].bitcast(I32))

            def front(b):
                pe.wait_ge(x_loaded, b * 16 + 16)
                for k in range(KD):
                    wait_attn_bank(pe, J_XT + k, b)
                    for t in range(TT):
                        mm = nc.tensor.transpose(apsum[(J_XT + k) % BANKS][:, t * P:(t + 1) * P],
                                                 xt[:, t, k * P:(k + 1) * P], ident[:])
                    mm.then_inc(pe_front, 1)
                pe.wait_ge(xT_ready, b * KD + KD)

                def in_proj(job, col):
                    wait_attn_bank(pe, job, b)
                    for k in range(KD):
                        mm = nc.tensor.matmul(apsum[job % BANKS][:], inw[:, k, col * P:(col + 1) * P], xT[:, k, :],
                                              start=(k == 0), stop=(k == KD - 1))
                    mm.then_inc(pe_front, 1)

                for c in range(DC):
                    in_proj(J_XX + c, c)
                wait_attn_bank(pe, J_DBL, b)
                pe.wait_ge(u_ready, b * DC + DC)
                for c in range(DC):
                    mm = nc.tensor.matmul(apsum[J_DBL % BANKS][0:DBL, :], xprojw[:, c, :], u[:, c, :],
                                          start=(c == 0), stop=(c == DC - 1))
                mm.then_inc(pe_front, 1)
                for c in range(DC):
                    in_proj(J_RES + c, DC + c)
                pe.wait_ge(xdbl_ready, b + 1)
                for c in range(DC):
                    wait_attn_bank(pe, J_DT + c, b)
                    nc.tensor.matmul(apsum[(J_DT + c) % BANKS][:], dtw[:, c * P:(c + 1) * P], xdbl[0:RANK, :],
                                     start=True, stop=True).then_inc(pe_front, 1)

            def tail(b):
                pe.wait_ge(y_gated, b + 1)
                for i in range(2):
                    wait_attn_bank(pe, J_OUT + i, b)
                    for h in range(2):
                        t = 2 * i + h
                        for c in range(DC):
                            mm = nc.tensor.matmul(apsum[(J_OUT + i) % BANKS][:, h * DIM:(h + 1) * DIM],
                                                  y[:, c, t * P:(t + 1) * P], outw[:, c, :],
                                                  start=(c == 0), stop=(c == DC - 1))
                    mm.then_inc(pe_tail, 1)
                pe.wait_ge(x1_ready, b * TT + TT)
                for k in range(KD):
                    wait_attn_bank(pe, J_X1T + k, b)
                    for t in range(TT):
                        mm = nc.tensor.transpose(apsum[(J_X1T + k) % BANKS][:, t * P:(t + 1) * P],
                                                 x1[:, t, k * P:(k + 1) * P], ident[:])
                    mm.then_inc(pe_tail, 1)

            def wait_ring(f, slot, parts):
                for e in range(slot * parts, (slot + 1) * parts):
                    loads = len(range(e % RING, SLOTS * parts, RING))
                    pe.wait_ge(ring_loaded[e % RING], f * (16 * loads) + 16 * (e // RING + 1))

            def ffn(f, parts):
                pe.wait_ge(x1_lo, f * KD + KD)
                for slot in range(L1_SLOTS):
                    wait_ring(f, slot, parts)
                    for q in range(4):
                        job = 4 * slot + q
                        if job >= BANKS:
                            if job % 2:
                                pe.wait_ge(l1_x32, f * HC + (job - BANKS) // 2 + 1)
                            else:
                                pe.wait_ge(l1_gate, f * HC + (job - BANKS) // 2 + 1)
                        steps = [(p, k, a) for p in range(parts) for k in range(KD) for a in (x1T_hi, x1T_lo)]
                        for n, (p, k, a) in enumerate(steps):
                            w = ring[:, (slot * parts + p) % RING, (q * KD + k) * P:(q * KD + k + 1) * P]
                            mm = nc.tensor.matmul(fpsum[job % BANKS][:], w, a[:, k, :],
                                                  start=(n == 0), stop=(n == len(steps) - 1))
                        mm.then_inc(pe_l1, 1)
                for i in range(2 * HC):
                    src_hi, src_lo = (ha_hi, ha_lo) if i < HC else (hb_hi, hb_lo)
                    if i % HC == 0:
                        pe.wait_ge(ffn_lo, f * (3 * HC) + HC * (1 + i // HC))
                    slot = L1_SLOTS + i
                    wait_ring(f, slot, parts)
                    job = 2 * HC + i
                    if i < BANKS:
                        if job % 2:
                            pe.wait_ge(l1_x32, f * HC + (job - BANKS) // 2 + 1)
                        else:
                            pe.wait_ge(l1_gate, f * HC + (job - BANKS) // 2 + 1)
                    else:
                        pe.wait_ge(gelu_x32, f * (2 * HC) + (i - BANKS + 1))
                    steps = [(p, k, a) for p in range(parts) for k in range(HC) for a in (src_hi, src_lo)]
                    for n, (p, k, a) in enumerate(steps):
                        w = ring[:, (slot * parts + p) % RING, k * P:(k + 1) * P]
                        mm = nc.tensor.matmul(fpsum[job % BANKS][:], w, a[:, k, :],
                                              start=(n == 0), stop=(n == len(steps) - 1))
                    mm.then_inc(pe_hid, 1)
                pe.wait_ge(ffn_lo, f * (3 * HC) + 3 * HC)
                for h in range(W3_SLOTS):
                    wait_ring(f, L1_SLOTS + 2 * HC + h, parts)
                for i in range(2):
                    job = 4 * HC + i
                    pe.wait_ge(gelu_x32, f * (2 * HC) + (2 * HC - BANKS + i + 1))
                    for h in range(2):
                        t = 2 * i + h
                        steps = [(p, k, a) for p in range(parts) for k in range(HC) for a in (ha_hi, ha_lo)]
                        for n, (p, k, a) in enumerate(steps):
                            slot = L1_SLOTS + 2 * HC + k // 4
                            w = ring[:, (slot * parts + p) % RING, (k % 4) * DIM:(k % 4 + 1) * DIM]
                            mm = nc.tensor.matmul(fpsum[job % BANKS][:, h * DIM:(h + 1) * DIM],
                                                  a[:, k, t * P:(t + 1) * P], w,
                                                  start=(n == 0), stop=(n == len(steps) - 1))
                    mm.then_inc(pe_w3, 1)

            def program(parts):
                with pe.Fori(1, BATCH) as b:
                    front(b)
                    ffn(b - 1, parts)
                    tail(b)
                ffn(BATCH - 1, parts)

            front(0)
            tail(0)
            with pe.If(general > 0):
                program(2)
            with pe.Else():
                program(1)

        @block.scalar
        def _(act):
            act.wait_ge(const_loaded, 16 * CONST_LOADS)
            nc.scalar.activation(a_neg[:], ch[:, :, C_ALOG:], ACT.Exp).then_inc(const_exp, 1)

            def split_slot(i, s):
                act.wait_ge(raw_loaded[s], 16 * i + 16)
                nc.scalar.activation(split_hi[:, s, :], raw[:, s, :], ACT.Copy).then_inc(split_hi_done, 1)
                act.wait_ge(split_lo_done, 2 * i + (s + 1))
                nc.scalar.activation(raw[:, s, :], split_lo[:, s, :].bitcast(F32), ACT.Abs,
                                     accum_out=low_sums[:, bass.ds(2 * i + s, 1)]).then_inc(split_sum_done, 1)

            for s in range(2):
                split_slot(0, s)
            with act.Fori(1, SLOTS // 2) as i:
                for s in range(2):
                    act.wait_ge(split_stored[s], 32 * i)
                    split_slot(i, s)

            def load_bc(b, n):
                if not (isinstance(b, int) and b == 0 and n < BC_RING):
                    last = (n - BC_RING + 1) * DC
                    act.wait_ge(hC_done, b * TILES + last)
                act.dma_start(bc[:, n % BC_RING], bc_dram[b].rearrange("(r n) l -> n r l", n=STATES)[n]
                              .partition_broadcast(P)).then_inc(bc_loaded[n % BC_RING], 16)

            def front(b):
                for k in range(KD):
                    act.wait_ge(pe_front, b * FRONT_JOBS + (J_XT + k + 1))
                    nc.scalar.activation(xT[:, k, :], apsum[(J_XT + k) % BANKS][:], ACT.Copy).then_inc(xT_ready, 1)
                for c in range(DC):
                    act.wait_ge(pe_front, b * FRONT_JOBS + (J_XX + c + 1))
                    nc.scalar.activation(u[:, c, :], apsum[(J_XX + c) % BANKS][:], ACT.Identity,
                                         bias=conv_half[:, c, TAPS:], scale=conv_half[:, c, TAPS - 1:TAPS]
                                         ).then_inc(conv_base, 1)
                for c in range(DC):
                    act.wait_ge(conv_taps, b * (DC * (TAPS - 1)) + (DC * (TAPS - 2) + c + 1))
                    nc.scalar.activation(delta[:, c, :], u[:, c, :], ACT.Tanh).then_inc(u_tanh, 1)
                act.wait_ge(pe_front, b * FRONT_JOBS + (J_DBL + 1))
                nc.scalar.activation(xdbl[:], apsum[J_DBL % BANKS][0:DBL, :], ACT.Copy).then_inc(xdbl_ready, 1)
                for c in range(DC):
                    act.wait_ge(pe_front, b * FRONT_JOBS + (J_RES + c + 1))
                    nc.scalar.activation(v[:, c, :], apsum[(J_RES + c) % BANKS][:], ACT.Tanh).then_inc(v_tanh, 1)
                act.wait_ge(bc_stored, b * 16 + 16)
                for n in range(BC_RING):
                    load_bc(b, n)
                act.wait_ge(dt_ready, b * DC + DC)
                nc.scalar.activation(y[:], delta[:], ACT.Abs).then_inc(act_softplus, 1)
                act.wait_ge(act_softplus, b * 3 + 1)
                nc.scalar.activation(y[:], y[:], ACT.Exp, scale=-1.0).then_inc(act_softplus, 1)
                act.wait_ge(dve_softplus, b * 4 + 2)
                nc.scalar.activation(sp_w, sp_w, ACT.Ln).then_inc(act_softplus, 1)
                act.wait_ge(dve_softplus, b * 4 + 3)
                for c in range(DC):
                    nc.scalar.activation(y[:, c, :], u[:, c, :], ACT.Copy, scale=ch[:, c, C_D:C_D + 1]
                                         ).then_inc(y_init, 1)

            def exp_tile(b, s):
                n, c = s // DC, s % DC
                wait_attn_bank(act, J_TILE + s, b)
                nc.scalar.activation(apsum[(J_TILE + s) % BANKS][:], delta[:, c, :], ACT.Exp,
                                     scale=a_neg[:, c, n:n + 1]).then_inc(dA_ready, 1)
                if n + 2 >= BC_RING and n + 2 < STATES and c == DC - 1:
                    load_bc(b, n + 2)

            def l1_gate_tanh(f, o):
                act.wait_ge(pe_l1, f * 2 * HC + (2 * o + 1))
                if o >= 2:
                    act.wait_ge(l1_x32, f * HC + (o - 1))
                nc.scalar.activation(gate[:, o % 2, :], fpsum[2 * o % BANKS][:], ACT.Tanh,
                                     scale=s1_half[:, o:o + 1]).then_inc(l1_tanh, 1)

            def l1_split_hi(f, o):
                act.wait_ge(l1_x32, f * HC + (o + 1))
                nc.scalar.activation(ha_hi[:, o, :], x32[:, o % X32, :], ACT.Copy).then_inc(ffn_hi, 1)

            def gelu_phase(f, g):
                for i in range(g * GELU_PHASE, (g + 1) * GELU_PHASE):
                    act.wait_ge(pe_hid, f * 2 * HC + (i + 1))
                    act.wait_ge(ffn_lo, f * (3 * HC) + (HC + i - X32 + 1))
                    nc.scalar.activation(x32[:, (HC + i) % X32, :], fpsum[(2 * HC + i) % BANKS][:], ACT.Gelu,
                                         scale=fs[:, 2 + i // HC, i % HC:i % HC + 1]).then_inc(gelu_x32, 1)
                for i in range(g * GELU_PHASE, (g + 1) * GELU_PHASE):
                    act.wait_ge(gelu_x32, f * 2 * HC + (i + 1))
                    if i == HC:
                        act.wait_ge(pe_hid, f * 2 * HC + HC)
                    dst = hb_hi if i < HC else ha_hi
                    nc.scalar.activation(dst[:, i % HC, :], x32[:, (HC + i) % X32, :], ACT.Copy).then_inc(ffn_hi, 1)

            def tail(b):
                for k in range(KD):
                    act.wait_ge(pe_tail, b * TAIL_JOBS + (2 + k + 1))
                    nc.scalar.activation(x1T_hi[:, k, :], apsum[(J_X1T + k) % BANKS][:], ACT.Copy).then_inc(x1_hi, 1)

            def between(f, s):
                o2 = s - L1_AT
                if 0 <= o2 < 2 * HC and o2 % 2 == 0:
                    l1_gate_tanh(f, o2 // 2)
                o2 = s - L1_AT - 4
                if 0 <= o2 < 2 * HC and o2 % 2 == 0:
                    l1_split_hi(f, o2 // 2)
                if s in GELU_AT:
                    gelu_phase(f, GELU_AT.index(s))

            act.wait_ge(const_dve, CONST_DVE)
            front(0)
            act.wait_ge(dve_softplus, 4)
            for s in range(TILES):
                exp_tile(0, s)
            tail(0)
            with act.Fori(1, BATCH) as b:
                front(b)
                act.wait_ge(dve_softplus, b * 4 + 4)
                for s in range(TILES):
                    between(b - 1, s)
                    exp_tile(b, s)
                tail(b)
            for s in range(TILES):
                between(BATCH - 1, s)

        @block.vector
        def _(dve):
            dve.wait_ge(const_loaded, 16 * CONST_LOADS)
            nc.vector.memset(ones[:], 1.0).then_inc(const_dve, 1)
            nc.vector.memset(eps[:], EPS).then_inc(const_dve, 1)
            nc.vector.memset(minus_half[:], -0.5).then_inc(const_dve, 1)
            nc.vector.tensor_scalar(conv_half[:], ch[:, :, 0:TAPS + 1], 0.5, None, ALU.mult).then_inc(const_dve, 1)
            nc.vector.tensor_scalar(inw[:, :, INNER:], inw[:, :, INNER:], 0.5, None, ALU.mult).then_inc(const_dve, 1)
            nc.vector.tensor_scalar(s1_half[:], fs[:, 0, :], 0.5, None, ALU.mult).then_inc(const_dve, 1)
            dve.wait_ge(const_exp, 1)
            nc.vector.tensor_scalar(a_neg[:], a_neg[:], -1.0, None, ALU.mult).then_inc(const_dve, 1)
            dve.wait_ge(const_dve, CONST_DVE)
            nc.vector.tensor_tensor(s12_half[:], s1_half[:], fs[:, 1, :], ALU.mult).then_inc(const_pool, 1)

            with dve.Fori(0, SLOTS // 2) as i:
                for s in range(2):
                    dve.wait_ge(split_hi_done, 2 * i + (s + 1))
                    nc.vector.tensor_tensor(split_lo[:, s, :], raw[:, s, :], split_hi[:, s, :].bitcast(F32),
                                            ALU.subtract).then_inc(split_lo_done, 1)
            dve.wait_ge(split_sum_done, SLOTS)
            nc.vector.tensor_reduce(low_sum[:], low_sums[:], mybir.AxisListType.X, ALU.add).then_inc(low_summed, 1)
            dve.wait_ge(low_total, 1)
            nc.vector.tensor_copy(low_flag[:], fpsum[0][0:1, 0:1]).then_inc(flag_ready, 1)

            def front(b):
                for n, tap in enumerate(range(TAPS - 2, -1, -1)):
                    back = TAPS - 1 - tap
                    for c in range(DC):
                        if n == 0:
                            dve.wait_ge(conv_base, b * DC + (c + 1))
                        else:
                            dve.wait_ge(conv_taps, b * (DC * (TAPS - 1)) + (DC * (n - 1) + c + 1))
                        nc.vector.scalar_tensor_tensor(
                            out=u[:, c, back:], in0=apsum[(J_XX + c) % BANKS][:, 0:SEQ - back],
                            scalar=conv_half[:, c, tap:tap + 1], in1=u[:, c, back:],
                            op0=ALU.mult, op1=ALU.add).then_inc(conv_taps, 1)
                for c in range(DC):
                    dve.wait_ge(u_tanh, b * DC + (c + 1))
                    nc.vector.scalar_tensor_tensor(out=u[:, c, :], in0=delta[:, c, :], scalar=1.0, in1=u[:, c, :],
                                                   op0=ALU.add, op1=ALU.mult).then_inc(u_ready, 1)
                for c in range(DC):
                    dve.wait_ge(v_tanh, b * DC + (c + 1))
                    nc.vector.scalar_tensor_tensor(out=v[:, c, :], in0=v[:, c, :], scalar=1.0,
                                                   in1=apsum[(J_RES + c) % BANKS][:],
                                                   op0=ALU.add, op1=ALU.mult).then_inc(v_ready, 1)
                for c in range(DC):
                    dve.wait_ge(pe_front, b * FRONT_JOBS + (J_DT + c + 1))
                    nc.vector.tensor_scalar(delta[:, c, :], apsum[(J_DT + c) % BANKS][:], ch[:, c, C_DTB:C_DTB + 1],
                                            None, ALU.add).then_inc(dt_ready, 1)
                dve.wait_ge(act_softplus, b * 3 + 2)
                nc.vector.tensor_scalar(sp_w, y[:], 1.0, None, ALU.add).then_inc(dve_softplus, 1)
                dve.wait_ge(dve_softplus, b * 4 + 1)
                nc.vector.scalar_tensor_tensor(out=y[:], in0=sp_w, scalar=1.0, in1=y[:],
                                               op0=ALU.subtract, op1=ALU.subtract).then_inc(dve_softplus, 1)
                dve.wait_ge(dve_softplus, b * 4 + 2)
                nc.vector.scalar_tensor_tensor(out=delta[:], in0=delta[:], scalar=0.0, in1=y[:],
                                               op0=ALU.max, op1=ALU.subtract).then_inc(dve_softplus, 1)
                dve.wait_ge(dve_softplus, b * 4 + 3)
                dve.wait_ge(act_softplus, b * 3 + 3)
                nc.vector.tensor_tensor(delta[:], delta[:], sp_w, ALU.add).then_inc(dve_softplus, 1)
                dve.wait_ge(dve_softplus, b * 4 + 4)
                dve.wait_ge(y_init, b * DC + DC)
                nc.vector.tensor_tensor(u[:], u[:], delta[:], ALU.mult).then_inc(du_ready, 1)

            def scan_tile(b, s):
                bank = apsum[(J_TILE + s) % BANKS]
                dve.wait_ge(dA_ready, b * TILES + (s + 1))
                dve.wait_ge(dBu_ready, b * TILES + (s + 1))
                nc.vector.tensor_tensor_scan(bank[:], bank[:], work[:, s % WORK, :], 0.0,
                                             ALU.mult, ALU.add).then_inc(scan_done, 1)

            def c_tile(b, s):
                n = s // DC
                dve.wait_ge(scan_done, b * TILES + (s + 1))
                nc.vector.tensor_tensor(work[:, s % WORK, :], apsum[(J_TILE + s) % BANKS][:],
                                        bc[:, n % BC_RING, 1, :], ALU.mult).then_inc(hC_done, 1)

            def l1_tile(f, o):
                dve.wait_ge(l1_tanh, f * HC + (o + 1))
                nc.vector.scalar_tensor_tensor(out=gate[:, o % 2, :], in0=gate[:, o % 2, :], scalar=1.0,
                                               in1=fpsum[2 * o % BANKS][:], op0=ALU.add, op1=ALU.mult
                                               ).then_inc(l1_gate, 1)
                dve.wait_ge(l1_gate, f * HC + (o + 1))
                dve.wait_ge(pe_l1, f * 2 * HC + (2 * o + 2))
                if o >= X32:
                    dve.wait_ge(ffn_lo, f * (3 * HC) + (o - X32 + 1))
                nc.vector.scalar_tensor_tensor(out=x32[:, o % X32, :], in0=gate[:, o % 2, :],
                                               scalar=s12_half[:, o:o + 1], in1=fpsum[(2 * o + 1) % BANKS][:],
                                               op0=ALU.mult, op1=ALU.mult).then_inc(l1_x32, 1)

            def layernorm(src, dst, seq, ready, done):
                for t in range(TT):
                    dve.wait_ge(ready[0], ready[1][t])
                    nc.vector.bn_stats(stats[:, t, :], src[:, t, :]).then_inc(ln_stats, 1)
                dve.wait_ge(ln_stats, seq * TT + TT)
                nc.vector.tensor_copy(stats_seen[:], stats[:, TT - 1, 0:1])
                for t in range(TT):
                    nc.vector.bn_aggr(mv[:, t, :], stats[:, t, :]).then_inc(ln_aggr, 1)
                dve.wait_ge(ln_rstd, seq + 1)
                for t in range(TT):
                    nc.vector.tensor_scalar(dst[:, t, :], src[:, t, :], mv[:, t, 0:1], rstd[:, t:t + 1],
                                            ALU.subtract, ALU.mult).then_inc(done, 1)

            def ffn_end(f, seq):
                for i in range(2):
                    dve.wait_ge(pe_w3, f * 2 + (i + 1))
                    dve.wait_ge(out_stored, f * 16 + 16)
                    nc.vector.tensor_tensor(out_st[:, 2 * i:2 * i + 2, :],
                                            fpsum[(4 * HC + i) % BANKS][:].rearrange("p (t d) -> p t d", t=2),
                                            w3s[:].unsqueeze(1).to_broadcast([P, 2, DIM]), ALU.mult
                                            ).then_inc(w3_scaled, 1)
                for i in range(2):
                    dve.wait_ge(w3_scaled, f * 2 + (i + 1))
                    nc.vector.tensor_tensor(out_st[:, 2 * i:2 * i + 2, :], out_st[:, 2 * i:2 * i + 2, :],
                                            x1[:, 2 * i:2 * i + 2, :], ALU.add).then_inc(z2_ready, 1)
                layernorm(out_st, out_st, seq, (z2_ready, [f * 2 + (t // 2 + 1) for t in range(TT)]), out_ready)

            def tail(b, seq):
                dve.wait_ge(y_added, b * TILES + TILES)
                nc.vector.tensor_tensor(y[:], y[:], v[:], ALU.mult).then_inc(y_gated, 1)
                for i in range(2):
                    dve.wait_ge(pe_tail, b * TAIL_JOBS + (i + 1))
                    nc.vector.tensor_tensor(xt[:, 2 * i:2 * i + 2, :],
                                            apsum[(J_OUT + i) % BANKS][:].rearrange("p (t d) -> p t d", t=2),
                                            xt[:, 2 * i:2 * i + 2, :], ALU.add).then_inc(z_ready, 1)
                layernorm(xt, x1, seq, (z_ready, [b * 2 + (t // 2 + 1) for t in range(TT)]), x1_ready)
                for k in range(KD):
                    dve.wait_ge(x1_hi, b * KD + (k + 1))
                    nc.vector.tensor_tensor(x1T_lo[:, k, :], apsum[(J_X1T + k) % BANKS][:],
                                            x1T_hi[:, k, :].bitcast(F32), ALU.subtract).then_inc(x1_lo, 1)

            def between(f, s):
                o2 = s - L1_AT
                if 0 <= o2 < 2 * HC and o2 % 2 == 0:
                    l1_tile(f, o2 // 2)

            front(0)
            for s in range(TILES + 1):
                if s < TILES:
                    scan_tile(0, s)
                if s >= 1:
                    c_tile(0, s - 1)
            tail(0, 0)
            with dve.Fori(1, BATCH) as b:
                front(b)
                for s in range(TILES + 1):
                    if s < TILES:
                        scan_tile(b, s)
                    if s >= 1:
                        c_tile(b, s - 1)
                    between(b - 1, s)
                ffn_end(b - 1, 2 * b - 1)
                tail(b, 2 * b)
            for s in range(TILES):
                between(BATCH - 1, s)
            ffn_end(BATCH - 1, 2 * BATCH - 1)

        @block.gpsimd
        def _(pool):
            pool.wait_ge(const_dve, CONST_DVE)

            def b_tile(b, s):
                n, c = s // DC, s % DC
                if c == 0:
                    pool.wait_ge(bc_loaded[n % BC_RING],
                                 b * (16 * STATES // BC_RING) + 16 * (n // BC_RING + 1))
                if s >= WORK:
                    pool.wait_ge(y_added, b * TILES + (s - WORK + 1))
                nc.gpsimd.tensor_tensor(work[:, s % WORK, :], u[:, c, :], bc[:, n % BC_RING, 0, :],
                                        ALU.mult).then_inc(dBu_ready, 1)

            def y_tile(b, s):
                c = s % DC
                pool.wait_ge(hC_done, b * TILES + (s + 1))
                if s >= DC:
                    pool.wait_ge(y_added, b * TILES + (s - DC + 1))
                nc.gpsimd.tensor_tensor(y[:, c, :], y[:, c, :], work[:, s % WORK, :], ALU.add).then_inc(y_added, 1)

            def split_lo_tile(f, i):
                pool.wait_ge(ffn_hi, f * (3 * HC) + (i + 1))
                hi, lo = (hb_hi, hb_lo) if HC <= i < 2 * HC else (ha_hi, ha_lo)
                nc.gpsimd.tensor_tensor(lo[:, i % HC, :], x32[:, i % X32, :], hi[:, i % HC, :].bitcast(F32),
                                        ALU.subtract).then_inc(ffn_lo, 1)

            def rstd_of(seq):
                pool.wait_ge(ln_aggr, seq * TT + TT)
                nc.gpsimd.tensor_tensor(var_eps[:], mv[:, :, 1], eps[:], ALU.add).then_inc(ln_eps, 1)
                pool.wait_ge(ln_eps, seq + 1)
                nc.gpsimd.tensor_tensor(rstd[:], var_eps[:], minus_half[:], ALU.pow).then_inc(ln_rstd, 1)

            def between(f, s):
                o2 = s - L1_AT - 4
                if 0 <= o2 < 2 * HC and o2 % 2 == 0:
                    split_lo_tile(f, o2 // 2)
                for g, at in enumerate(GELU_AT):
                    k = s - (at - GELU_PHASE + 1)
                    if 0 <= k < GELU_PHASE:
                        split_lo_tile(f, HC + g * GELU_PHASE + k)

            def scan_of(b, f):
                pool.wait_ge(du_ready, b + 1)
                for s in range(TILES + LEAD):
                    if s < TILES:
                        b_tile(b, s)
                    if s >= LEAD:
                        if f is not None:
                            between(f, s - LEAD)
                        y_tile(b, s - LEAD)

            scan_of(0, None)
            rstd_of(0)
            with pool.Fori(1, BATCH) as b:
                scan_of(b, b - 1)
                rstd_of(2 * b - 1)
                rstd_of(2 * b)
            for s in range(TILES):
                between(BATCH - 1, s)
            rstd_of(2 * BATCH - 1)


def kernel(L0_attn_x, L0_attn_in_w, L0_attn_conv_w, L0_attn_conv_b, L0_attn_xproj_w, L0_attn_dt_w, L0_attn_dt_b,
           L0_attn_A_log, L0_attn_D, L0_attn_out_w, L0_ffn_w1_w, L0_ffn_w1_s, L0_ffn_w2_w, L0_ffn_w2_s,
           L0_ffn_h1_w, L0_ffn_h1_s, L0_ffn_h2_w, L0_ffn_h2_s, L0_ffn_w3_w, L0_ffn_w3_s):
    import numpy as np
    import concourse.bacc as bacc
    from concourse.bass_utils import run_bass_kernel_spmd

    def ktiles(wT):
        return wT.reshape(-1, P, wT.shape[1]).transpose(1, 0, 2)

    def channels(a):
        return a.reshape(-1, P, a.shape[1]).transpose(1, 0, 2)

    A = np.asarray
    chan = np.concatenate([channels(A(L0_attn_conv_w)[:, 0, :])]
                          + [channels(A(a)[:, None]) for a in (L0_attn_conv_b, L0_attn_D, L0_attn_dt_b)]
                          + [channels(A(L0_attn_A_log))], axis=2)
    w1, w2, h1, h2, w3 = (ktiles(A(w).T) for w in (L0_ffn_w1_w, L0_ffn_w2_w, L0_ffn_h1_w, L0_ffn_h2_w, L0_ffn_w3_w))
    slots = []
    for s in range(L1_SLOTS):
        tiles = [w[:, :, o * P:(o + 1) * P] for o in (2 * s, 2 * s + 1) for w in (w1, w2)]
        slots.append(np.concatenate(tiles, axis=1).reshape(P, SLOT_COLS))
    for w in (h1, h2):
        slots += [w[:, :, o * P:(o + 1) * P].reshape(P, SLOT_COLS) for o in range(HC)]
    slots += [w3[:, 4 * h:4 * h + 4, :].reshape(P, SLOT_COLS) for h in range(W3_SLOTS)]
    scales = np.concatenate([channels(A(s)[:, None]).transpose(0, 2, 1)
                             for s in (L0_ffn_w1_s, L0_ffn_w2_s, L0_ffn_h1_s, L0_ffn_h2_s)], axis=1)
    arrays = {
        "x_tok": A(L0_attn_x).reshape(BATCH, TT, P, DIM).transpose(0, 2, 1, 3),
        "in_wT": ktiles(A(L0_attn_in_w).T),
        "chan": chan,
        "xproj_wT": ktiles(A(L0_attn_xproj_w).T),
        "dt_wT": A(L0_attn_dt_w).T,
        "out_wT": ktiles(A(L0_attn_out_w).T),
        "ffn_w": np.stack(slots),
        "ffn_s": scales,
        "w3_s": A(L0_ffn_w3_s),
        "identity": np.eye(P, dtype=np.float32),
    }
    arrays = {n: np.ascontiguousarray(a) for n, a in arrays.items()}
    nc = bacc.Bacc("TRN2", target_bir_lowering=False, num_devices=1)
    args = [nc.dram_tensor(n, list(a.shape), mybir.dt.from_np(a.dtype), kind="ExternalInput").ap()
            for n, a in arrays.items()]
    out = nc.dram_tensor("out_tok", [BATCH, P, TT, DIM], F32, kind="ExternalOutput").ap()
    build(nc, *args, out)
    r = run_bass_kernel_spmd(nc, [arrays], core_ids=[0])
    return r.results[0]["out_tok"].transpose(0, 2, 1, 3).reshape(BATCH, SEQ, DIM)
```

```python
from contextlib import ExitStack

import concourse.bass as bass
from concourse import mybir

F32 = mybir.dt.float32
F32R = mybir.dt.float32r
I32 = mybir.dt.int32
ALU = mybir.AluOpType
ACT = mybir.ActivationFunctionType

P = 128
BATCH, SEQ, DIM = 16, 512, 256
INNER, STATES, RANK, TAPS, HIDDEN = 512, 16, 16, 4, 1024
KD = DIM // P
DC = INNER // P
HC = HIDDEN // P
TT = SEQ // P
TILES = STATES * DC
PAIRS = TILES // 2
DTC = RANK + STATES
EPS = 1e-5

C_CONVB, C_D, C_DTB, C_ALOG = TAPS, TAPS + 1, TAPS + 2, TAPS + 3
CHAN = TAPS + 3 + STATES

L1_SLOTS, W3_SLOTS = HC // 2, 2
SLOTS = L1_SLOTS + 2 * HC + W3_SLOTS
SLOT_COLS = HC * P
ENTRY_COLS = SLOT_COLS // 2
RING = 4
HALVES = 4 * HC
QUARTERS = 2 * W3_SLOTS

T_XT, T_RES, T_OUT, T_ADD, T_STATS, T_NORM, T_X1T = (0, 1), (1, 3, 5, 7), (10, 11, 13, 14), (12, 15), 16, 17, (18, 19)
E_W3, E_SCALE, E_ADD, E_STATS, E_NORM = (9, 10, 11, 12), (11, 13), (12, 14), 15, 16
A_L1 = 20
A_HI, A_LO = 2, 3
HALF_AT = [31, 32, 33, 34, 35, 36, 38, 39, 40, 41, 42, 43, 45, 46, 47, 48,
           52, 53, 54, 55, 56, 57, 59, 60, 61, 62, 63, 64, 66, 67, 68, 69]
GELU_AT = {37: (0, 1, 2), 44: (3, 4, 5), 49: (6, 7), 58: (8, 9, 10), 65: (11, 12, 13), 70: (14, 15)}
HI_AT = {38: (0,), 39: (1,), 40: (2,), 45: (3,), 46: (4,), 47: (5,), 50: (6, 7),
         59: (8,), 60: (9,), 61: (10,), 66: (11,), 67: (12,), 68: (13,), 71: (14, 15)}
LO_AFTER = 1
F_XT, F_XX, F_DBL, F_DBL_OUT, F_BT, F_BT_OUT = (22, 24), (28, 30, 32, 34), 37, 38, 39, 40
F_DT, F_LN, F_DELTA, F_DELTA_U, F_Y, F_DU = (41, 42, 43, 44), 49, (50, 50, 51, 51), (51, 52, 53, 54), (52, 53, 54, 55), (
    57, 58, 59, 60)
EXP_LEAD, B_LEAD, SCALE_LEAD = 3, 2, 6
PREP_AT = {2 * k: k for k in range(SLOTS)}
X32 = 4
SPLITS = 4


def build(nc, x, in_wT, chan, xproj_wT, dt_wT, out_wT, ffn_w, ffn_s, w3_s, ident_in, out):
    c_dram = nc.dram_tensor("c_rows", [BATCH, STATES, SEQ], F32, kind="Internal").ap()
    w_dram = nc.dram_tensor("split_weights", [2, SLOTS, P, SLOT_COLS], F32, kind="Internal").ap()

    with ExitStack() as ctx:
        def sb(name, shape, dt=F32):
            return ctx.enter_context(nc.sbuf_tensor(name, shape, dt))

        def sem(name):
            return ctx.enter_context(nc.semaphore(name))

        ident = sb("ident", [P, P])
        inw = sb("inw", [P, KD, 2 * INNER])
        outw = sb("outw", [P, DC, DIM])
        xprojw = sb("xprojw", [P, DC, DTC + STATES])
        dtw = sb("dtw", [RANK, INNER])
        ch = sb("ch", [P, DC, CHAN])
        fs = sb("fs", [P, 4, HC])
        w3s = sb("w3s", [P, DIM])
        conv_half = sb("conv_half", [P, DC, TAPS + 1])
        a_neg = sb("a_neg", [P, DC, STATES])
        s1_half = sb("s1_half", [P, HC])
        s12_half = sb("s12_half", [P, HC])
        minus_half = sb("minus_half", [P, TT])
        eps = sb("eps", [P, TT])
        ones = sb("ones", [P, 1])
        low_sums = sb("low_sums", [P, SLOTS])
        low_sum = sb("low_sum", [P, 1])
        low_flag = sb("low_flag", [1, 1])
        xf = sb("xf", [P, TT, DIM])
        xt = sb("xt", [P, TT, DIM])
        xT = sb("xT", [P, KD, SEQ])
        y2 = sb("y2", [P, 2, DC, SEQ])
        delta2 = sb("delta2", [P, 2, DC, SEQ])
        bT2 = sb("bT2", [P, 2, TT, STATES])
        du = sb("du", [P, DC, SEQ])
        duT = sb("duT", [P, TT, INNER])
        c_rows = sb("c_rows_sb", [P, 2, SEQ])
        dB = sb("dB", [P, 2, TT, INNER])
        dA = sb("dA", [P, 4, SEQ])
        hC = sb("hC", [P, 2, 2, SEQ])
        ring = sb("ring", [P, RING, ENTRY_COLS], F32R)
        x1 = sb("x1", [P, TT, DIM])
        ha_hi = sb("ha_hi", [P, HC, SEQ], F32R)
        ha_lo = sb("ha_lo", [P, HC, SEQ], F32R)
        hb_hi = sb("hb_hi", [P, HC, SEQ], F32R)
        hb_lo = sb("hb_lo", [P, HC, SEQ], F32R)
        gate = sb("gate", [P, 2, SEQ])
        x32 = sb("x32", [P, X32, SEQ])
        out_st = sb("out_st", [P, TT, DIM])
        stats = sb("stats", [P, 2, TT, 6])
        stats_seen = sb("stats_seen", [P, 2])
        mv = sb("mv", [P, 2, TT, 2])
        var_eps = sb("var_eps", [P, 2, TT])
        rstd = sb("rstd", [P, 2, TT])

        xdbl = xT[0:DTC, 0, :]
        x1T_hi, x1T_lo = hb_hi[:, 0:KD, :], hb_lo[:, 0:KD, :]
        sp_w = [out_st[:, 2 * c:2 * c + 2, :].rearrange("p t d -> p (t d)") for c in range(2)] + [
            gate[:, c, :] for c in range(2)]
        raw = x32[:].rearrange("p (s a) l -> p s (a l)", s=2)
        split_hi = ha_hi[:].rearrange("p (s a) l -> p s (a l)", s=SPLITS)
        split_lo = ha_lo[:].rearrange("p (s a) l -> p s (a l)", s=SPLITS)

        scan_ps = ctx.enter_context(nc.psum_tensor("scan_ps", [P, 4, SEQ], F32))
        ffn_ps = [ctx.enter_context(nc.psum_tensor(f"ffn_ps{i}", [P, SEQ], F32)) for i in range(3)]
        misc_ps = ctx.enter_context(nc.psum_tensor("misc_ps", [P, SEQ], F32))

        const_loaded = sem("const_loaded")
        raw_loaded = [sem(f"raw_loaded{i}") for i in range(2)]
        split_stored = [sem(f"split_stored{i}") for i in range(SPLITS)]
        xf_loaded = sem("xf_loaded")
        xr_loaded = sem("xr_loaded")
        c_stored = sem("c_stored")
        c_loaded = [sem(f"c_loaded{i}") for i in range(2)]
        ring_loaded = [sem(f"ring_loaded{i}") for i in range(RING)]
        out_stored = sem("out_stored")
        const_dve, const_exp, const_s12 = sem("const_dve"), sem("const_exp"), sem("const_s12")
        split_hi_done, split_lo_done = sem("split_hi_done"), sem("split_lo_done")
        split_sum_done, low_summed = sem("split_sum_done"), sem("low_summed")
        low_total, flag_ready = sem("low_total"), sem("flag_ready")
        pe_xT, pe_xx, pe_dbl, pe_bT = sem("pe_xT"), sem("pe_xx"), sem("pe_dbl"), sem("pe_bT")
        pe_dt, pe_duT, pe_dBu = sem("pe_dt"), sem("pe_duT"), sem("pe_dBu")
        pe_tail_xT, pe_res, pe_out, pe_x1T = sem("pe_tail_xT"), sem("pe_res"), sem("pe_out"), sem("pe_x1T")
        pe_l1, pe_half, pe_w3, pe_quarter = sem("pe_l1"), sem("pe_half"), sem("pe_w3"), sem("pe_quarter")
        xT_ready, conv_base, conv_taps = sem("xT_ready"), sem("conv_base"), sem("conv_taps")
        u_tanh, u_ready, xdbl_ready, bT_ready = sem("u_tanh"), sem("u_ready"), sem("xdbl_ready"), sem("bT_ready")
        dt_ready, sp_abs, sp_exp, sp_plus = sem("dt_ready"), sem("sp_abs"), sem("sp_exp"), sem("sp_plus")
        sp_lost, sp_ln, sp_max = sem("sp_lost"), sem("sp_ln"), sem("sp_max")
        delta_ready, du_ready, y_init = sem("delta_ready"), sem("du_ready"), sem("y_init")
        duT_ready = sem("duT_ready")
        dB_ready, dA_ready, scan_done = sem("dB_ready"), sem("dA_ready"), sem("scan_done")
        hC_done, y_added = sem("hC_done"), sem("y_added")
        tail_xT_ready, v_tanh, v_ready = sem("tail_xT_ready"), sem("v_tanh"), sem("v_ready")
        y_gated, z_ready = sem("y_gated"), sem("z_ready")
        x1_ready, x1_hi, x1_lo = sem("x1_ready"), sem("x1_hi"), sem("x1_lo")
        ln_stats = [sem(f"ln_stats{i}") for i in range(2)]
        ln_aggr = [sem(f"ln_aggr{i}") for i in range(2)]
        ln_eps = [sem(f"ln_eps{i}") for i in range(2)]
        ln_rstd = [sem(f"ln_rstd{i}") for i in range(2)]
        l1_tanh, l1_gate, l1_x32 = sem("l1_tanh"), sem("l1_gate"), sem("l1_x32")
        gelu_x32, ffn_hi, ffn_lo = sem("gelu_x32"), sem("ffn_hi"), sem("ffn_lo")
        w3_scaled, z2_ready, out_ready = sem("w3_scaled"), sem("z2_ready"), sem("out_ready")

        block = ctx.enter_context(nc.Block())

        CONST_LOADS, CONST_DVE = 8, 7
        FFN_TILES = 3 * HC

        def wait_past(eng, semaphore, value):
            if not (isinstance(value, int) and value <= 0):
                eng.wait_ge(semaphore, value)

        def rows(i, par):
            def row(k):
                if isinstance(i, int) and not 0 <= i + k < BATCH:
                    return None, None
                return i + k, (par + k) % 2
            return row(0), row(1), row(-1), row(-2)

        def main_loop(eng, iteration, *args):
            iteration(1, 1, *args)
            with eng.Fori(0, (BATCH - 4) // 2) as j:
                for h in range(2):
                    iteration(2 * j + (2 + h), h, *args)
            for i in range(BATCH - 2, BATCH + 2):
                iteration(i, i % 2, *args)

        def ring_entries(parts):
            halves = HC * parts
            w3 = halves + HALVES * parts
            return halves, w3, w3 + (QUARTERS if parts == 1 else TT * QUARTERS * parts)

        @block.sync
        def _(sp):
            for dst, src in ((ident[:], ident_in), (inw[:], in_wT), (ch[:], chan), (xprojw[:], xproj_wT),
                             (dtw[:], dt_wT), (outw[:], out_wT), (fs[:], ffn_s),
                             (w3s[:], w3_s.partition_broadcast(P))):
                sp.dma_start(dst, src).then_inc(const_loaded, 16)

            def load_front(r):
                wait_past(sp, pe_xT, r * KD)
                sp.dma_start(xf[:], x[r]).then_inc(xf_loaded, 16)

            def load_tail(i):
                wait_past(sp, x1_ready, i * TT)
                sp.dma_start(xt[:], x[i]).then_inc(xr_loaded, 16)

            def store_c(r):
                sp.wait_ge(xdbl_ready, r + 1)
                sp.dma_start(c_dram[r], xdbl[RANK:DTC, :]).then_inc(c_stored, 16)

            def store_parts(k):
                sp.wait_ge(split_lo_done, k + 1)
                for p, part in enumerate((split_hi, split_lo)):
                    sp.dma_start(w_dram[p, k], part[:, k % SPLITS, :].bitcast(F32)
                                 ).then_inc(split_stored[k % SPLITS], 16)

            def load_weights(f, entries, parts):
                first_half, first_w3, total = ring_entries(parts)
                for e in entries:
                    used = e - RING
                    if used < 0:
                        wait_past(sp, pe_w3, f * TT)
                    elif used < first_half:
                        sp.wait_ge(pe_l1, f * (2 * HC) + 2 * (used // parts + 1))
                    elif used < first_w3:
                        sp.wait_ge(pe_half, f * HALVES + ((used - first_half) // parts + 1))
                    else:
                        t, q = divmod((used - first_w3) // parts, QUARTERS)
                        if q == QUARTERS - 1:
                            sp.wait_ge(pe_w3, f * TT + (t + 1))
                        else:
                            sp.wait_ge(pe_quarter, f * (TT * (QUARTERS - 1)) + (t * (QUARTERS - 1) + q + 1))
                    if e < first_half:
                        half, part = divmod(e, parts)
                    elif e < first_w3:
                        half, part = divmod(e - first_half, parts)
                        half += HC
                    else:
                        half, part = divmod((e - first_w3) % (QUARTERS * parts), parts)
                        half += HC + HALVES
                    sp.dma_start(ring[:, e % RING, :].bitcast(F32),
                                 w_dram[part, half // 2][:, (half % 2) * ENTRY_COLS:(half % 2 + 1) * ENTRY_COLS]
                                 ).then_inc(ring_loaded[e % RING], 16)

            load_front(0)
            for k in range(2):
                sp.dma_start(raw[:, k, :], ffn_w[k]).then_inc(raw_loaded[k], 16)
            store_c(0)
            load_front(1)
            load_tail(0)
            for slot, k in PREP_AT.items():
                if slot == F_DBL_OUT + F_DBL_OUT % 2:
                    store_c(1)
                store_parts(k)
                if k + 2 < SLOTS:
                    sp.wait_ge(split_sum_done, k + 1)
                    sp.dma_start(raw[:, k % 2, :], ffn_w[k + 2]).then_inc(raw_loaded[k % 2], 16)
            for n in range(SPLITS):
                sp.wait_ge(split_stored[n], 32 * len(range(n, SLOTS, SPLITS)))
            sp.wait_ge(flag_ready, 1)
            general = sp.value_load(low_flag[0:1, 0:1].bitcast(I32))

            def iteration(i, par, parts):
                (_, _), (front, _), (tail, _), (end, _) = rows(i, par)
                first_half, first_w3, total = ring_entries(parts)
                if front is not None:
                    load_front(front)
                if end is not None:
                    load_weights(end, range(first_w3, total), parts)
                if tail is not None:
                    load_weights(tail, range(RING), parts)
                if end is not None:
                    sp.wait_ge(out_ready, end * TT + TT)
                    sp.dma_start(out[end], out_st[:]).then_inc(out_stored, 16)
                if tail is not None:
                    if not (isinstance(i, int) and i >= BATCH):
                        load_tail(i)
                    load_weights(tail, range(RING, first_half), parts)
                    mid = first_half + parts * sum(h < F_DBL_OUT for h in HALF_AT) + RING
                    load_weights(tail, range(first_half, mid), parts)
                    if front is not None:
                        store_c(front)
                    load_weights(tail, range(mid, first_w3), parts)

            with sp.If(general > 0):
                main_loop(sp, iteration, 2)
            with sp.Else():
                main_loop(sp, iteration, 1)
            sp.wait_ge(out_stored, 16 * BATCH)
            sp.wait_ge(c_stored, 16 * BATCH)

        @block.tensor
        def _(pe):
            pe.wait_ge(const_loaded, 16 * CONST_LOADS)
            pe.wait_ge(const_dve, CONST_DVE)

            def transposes(dst, src, n):
                for j in range(n):
                    mm = nc.tensor.transpose(dst[:, j * P:(j + 1) * P], src(j), ident[:])
                return mm

            def in_proj(col):
                for k in range(KD):
                    mm = nc.tensor.matmul(misc_ps[:], inw[:, k, col * P:(col + 1) * P], xT[:, k, :],
                                          start=(k == 0), stop=(k == KD - 1))
                return mm

            def b_tile(r, s):
                n, c = divmod(s, DC)
                if c == 0:
                    pe.wait_ge(dB_ready, r * (STATES * TT) + (n + 1) * TT)
                wait_past(pe, hC_done, r * PAIRS + ((s - 4) // 2 + 1))
                transposes(scan_ps[:, s % 4], lambda t: dB[:, n % 2, t, c * P:(c + 1) * P], TT
                           ).then_inc(pe_dBu, 1)

            def front_step(i, r, par, s, tail):
                if s in F_XT:
                    k = F_XT.index(s)
                    if k:
                        pe.wait_ge(xT_ready, r * KD + k)
                    else:
                        pe.wait_ge(xf_loaded, r * 16 + 16)
                        if tail is not None:
                            pe.wait_ge(x1_lo, tail * KD + KD)
                        else:
                            wait_past(pe, duT_ready, i * TT + TT)
                    transposes(misc_ps, lambda t: xf[:, t, k * P:(k + 1) * P], TT).then_inc(pe_xT, 1)
                if s in F_XX:
                    c = F_XX.index(s)
                    if c:
                        pe.wait_ge(conv_taps, r * (DC * (TAPS - 1)) + c * (TAPS - 1))
                    else:
                        pe.wait_ge(xT_ready, r * KD + KD)
                    in_proj(c).then_inc(pe_xx, 1)
                if s == F_DBL:
                    pe.wait_ge(u_ready, r * DC + DC)
                    for c in range(DC):
                        mm = nc.tensor.matmul(misc_ps[0:DTC, :], xprojw[:, c, 0:DTC], y2[:, par, c, :],
                                              start=(c == 0), stop=(c == DC - 1))
                    mm.then_inc(pe_dbl, 1)
                if s == F_BT:
                    pe.wait_ge(xdbl_ready, r + 1)
                    for t in range(TT):
                        for c in range(DC):
                            mm = nc.tensor.matmul(misc_ps[:, t * STATES:(t + 1) * STATES],
                                                  y2[:, par, c, t * P:(t + 1) * P], xprojw[:, c, DTC:],
                                                  start=(c == 0), stop=(c == DC - 1))
                    mm.then_inc(pe_bT, 1)
                if s in F_DT:
                    c = F_DT.index(s)
                    if c:
                        pe.wait_ge(dt_ready, r * DC + c)
                    else:
                        pe.wait_ge(bT_ready, r + 1)
                    nc.tensor.matmul(misc_ps[:], dtw[:, c * P:(c + 1) * P], xdbl[0:RANK, :],
                                     start=True, stop=True).then_inc(pe_dt, 1)
                if s in F_DU:
                    t = F_DU.index(s)
                    if t:
                        pe.wait_ge(duT_ready, r * TT + t)
                    else:
                        pe.wait_ge(du_ready, r * DC + DC)
                    transposes(misc_ps, lambda c: du[:, c, t * P:(t + 1) * P], DC).then_inc(pe_duT, 1)

            def tail_step(r, par, s):
                if s in T_XT:
                    k = T_XT.index(s)
                    if k:
                        pe.wait_ge(tail_xT_ready, r * KD + k)
                    elif isinstance(r, int) and r == BATCH - 1:
                        pe.wait_ge(x1_lo, r * KD)
                    else:
                        pe.wait_ge(duT_ready, r * TT + 2 * TT)
                    if not k:
                        pe.wait_ge(xr_loaded, r * 16 + 16)
                    transposes(misc_ps, lambda t: xt[:, t, k * P:(k + 1) * P], TT).then_inc(pe_tail_xT, 1)
                if s in T_RES:
                    c = T_RES.index(s)
                    if c:
                        pe.wait_ge(v_ready, r * DC + c)
                    else:
                        pe.wait_ge(tail_xT_ready, r * KD + KD)
                    in_proj(DC + c).then_inc(pe_res, 1)
                if s in T_OUT:
                    t = T_OUT.index(s)
                    if t == 0:
                        pe.wait_ge(y_gated, r * DC + DC)
                    if t == 2:
                        pe.wait_ge(z_ready, r * 2 + 1)
                    for c in range(DC):
                        mm = nc.tensor.matmul(misc_ps[:, (t % 2) * DIM:(t % 2 + 1) * DIM],
                                              y2[:, par, c, t * P:(t + 1) * P], outw[:, c, :],
                                              start=(c == 0), stop=(c == DC - 1))
                    mm.then_inc(pe_out, 1)
                if s in T_X1T:
                    k = T_X1T.index(s)
                    if k:
                        pe.wait_ge(x1_lo, r * KD + k)
                    else:
                        pe.wait_ge(x1_ready, r * TT + TT)
                    transposes(misc_ps, lambda t: x1[:, t, k * P:(k + 1) * P], TT).then_inc(pe_x1T, 1)

            def wait_entry(f, e, parts):
                per_row = ring_entries(parts)[2] // RING
                pe.wait_ge(ring_loaded[e % RING], f * (16 * per_row) + 16 * (e // RING + 1))

            def products(dst, steps, first, last):
                for n, (w, a) in enumerate(steps):
                    mm = nc.tensor.matmul(dst, w, a, start=(first and n == 0), stop=(last and n == len(steps) - 1))
                return mm

            def l1_tile(f, o, parts):
                if o == 0:
                    pe.wait_ge(x1_lo, f * KD + KD)
                for p in range(parts):
                    wait_entry(f, o * parts + p, parts)
                for q in range(2):
                    job = 2 * o + q
                    if job >= 3:
                        prev = job - 3
                        pe.wait_ge(l1_x32 if prev % 2 else l1_gate, f * HC + (prev // 2 + 1))
                    steps = [(ring[:, (o * parts + p) % RING, (q * KD + k) * P:(q * KD + k + 1) * P], a[:, k, :])
                             for p in range(parts) for k in range(KD) for a in (x1T_hi, x1T_lo)]
                    products(ffn_ps[job % 3][:], steps, True, True).then_inc(pe_l1, 1)

            def half_tile(f, m, parts):
                i, kh = divmod(m, 2)
                src = (ha_hi, ha_lo) if i < HC else (hb_hi, hb_lo)
                job = 2 * HC + i
                if kh == 0:
                    if i % HC == 0:
                        pe.wait_ge(ffn_lo, f * FFN_TILES + HC * (1 + i // HC))
                    prev = job - 3
                    if prev < 2 * HC:
                        pe.wait_ge(l1_x32 if prev % 2 else l1_gate, f * HC + (prev // 2 + 1))
                    else:
                        pe.wait_ge(gelu_x32, f * (2 * HC) + (prev - 2 * HC + 1))
                first_half = ring_entries(parts)[0]
                steps = []
                for p in range(parts):
                    e = first_half + m * parts + p
                    wait_entry(f, e, parts)
                    steps += [(ring[:, e % RING, k * P:(k + 1) * P], a[:, kh * HC // 2 + k, :])
                              for k in range(HC // 2) for a in src]
                products(ffn_ps[job % 3][:], steps, kh == 0, kh == 1).then_inc(pe_half, 1)

            def w3_tile(f, t, parts):
                job = 4 * HC + t // 2
                first_w3 = ring_entries(parts)[1]
                if t == 0:
                    pe.wait_ge(ffn_lo, f * FFN_TILES + 3 * HC)
                if t % 2 == 0:
                    pe.wait_ge(gelu_x32, f * (2 * HC) + (job - 3 - 2 * HC + 1))
                for q in range(QUARTERS):
                    steps = []
                    for p in range(parts):
                        e = first_w3 + (q if parts == 1 else (t * QUARTERS + q) * parts + p)
                        if parts > 1 or t == 0:
                            wait_entry(f, e, parts)
                        steps += [(a[:, 2 * q + k, t * P:(t + 1) * P], ring[:, e % RING, k * DIM:(k + 1) * DIM])
                                  for k in range(2) for a in (ha_hi, ha_lo)]
                    mm = products(ffn_ps[job % 3][:, (t % 2) * DIM:(t % 2 + 1) * DIM], steps, q == 0,
                                  q == QUARTERS - 1)
                    if q == QUARTERS - 1:
                        mm.then_inc(pe_w3, 1)
                    elif parts > 1:
                        mm.then_inc(pe_quarter, 1)

            def iteration(i, par, parts):
                (scan, _), (front, fpar), (tail, tpar), (end, _) = rows(i, par)
                for s in range(TILES):
                    if s + B_LEAD < TILES:
                        if scan is not None:
                            b_tile(scan, s + B_LEAD)
                    elif front is not None:
                        b_tile(front, s + B_LEAD - TILES)
                    if tail is not None:
                        tail_step(tail, tpar, s)
                    if front is not None:
                        front_step(i, front, fpar, s, tail)
                    if end is not None:
                        if s + TILES in HALF_AT:
                            half_tile(end, HALF_AT.index(s + TILES), parts)
                        if s in E_W3:
                            w3_tile(end, E_W3.index(s), parts)
                    if tail is not None:
                        if A_L1 <= s < A_L1 + HC:
                            l1_tile(tail, s - A_L1, parts)
                        if s in HALF_AT:
                            half_tile(tail, HALF_AT.index(s), parts)

            iteration(-1, 1, 1)
            iteration(0, 0, 1)
            pe.wait_ge(low_summed, 1)
            nc.tensor.matmul(ffn_ps[0][0:1, 0:1], low_sum[:], ones[:], start=True, stop=True).then_inc(low_total, 1)
            pe.wait_ge(flag_ready, 1)
            general = pe.value_load(low_flag[0:1, 0:1].bitcast(I32))
            with pe.If(general > 0):
                main_loop(pe, iteration, 2)
            with pe.Else():
                main_loop(pe, iteration, 1)

        @block.scalar
        def _(act):
            act.wait_ge(const_loaded, 16 * CONST_LOADS)
            nc.scalar.activation(a_neg[:], ch[:, :, C_ALOG:], ACT.Exp).then_inc(const_exp, 1)
            act.wait_ge(const_dve, CONST_DVE)

            def split_slot(k):
                act.wait_ge(raw_loaded[k % 2], 16 * (k // 2 + 1))
                if k >= SPLITS:
                    act.wait_ge(split_stored[k % SPLITS], 32 * (k // SPLITS))
                nc.scalar.activation(split_hi[:, k % SPLITS, :], raw[:, k % 2, :], ACT.Copy).then_inc(split_hi_done, 1)

            def sum_low(k):
                act.wait_ge(split_lo_done, k + 1)
                nc.scalar.activation(raw[:, k % 2, :], split_lo[:, k % SPLITS, :].bitcast(F32), ACT.Abs,
                                     accum_out=low_sums[:, k:k + 1]).then_inc(split_sum_done, 1)

            def load_c(r, n):
                wait_past(act, hC_done, r * PAIRS + 2 * (n - 1))
                act.wait_ge(c_stored, r * 16 + 16)
                act.dma_start(c_rows[:, n % 2], c_dram[r][n].partition_broadcast(P)).then_inc(c_loaded[n % 2], 16)

            def exp_tile(r, par, s):
                n, c = divmod(s, DC)
                if s == 0:
                    act.wait_ge(delta_ready, r * DC + DC)
                wait_past(act, scan_done, r * TILES + (s - 3))
                nc.scalar.activation(dA[:, s % 4], delta2[:, par, c, :], ACT.Exp, scale=a_neg[:, c, n:n + 1]
                                     ).then_inc(dA_ready, 1)

            def scale_tile(r, par, m):
                n, t = divmod(m, TT)
                if n == 0:
                    act.wait_ge(duT_ready, r * TT + (t + 1))
                if t == 0:
                    wait_past(act, pe_dBu, r * TILES + (n - 1) * DC)
                nc.scalar.activation(dB[:, n % 2, t, :], duT[:, t, :], ACT.Copy, scale=bT2[:, par, t, n:n + 1]
                                     ).then_inc(dB_ready, 1)

            def front_step(r, par, s):
                if s in F_XT:
                    k = F_XT.index(s)
                    act.wait_ge(pe_xT, r * KD + (k + 1))
                    nc.scalar.activation(xT[:, k, :], misc_ps[:], ACT.Copy).then_inc(xT_ready, 1)
                if s - 1 in F_XX:
                    c = F_XX.index(s - 1)
                    act.wait_ge(pe_xx, r * DC + (c + 1))
                    nc.scalar.activation(y2[:, par, c, :], misc_ps[:], ACT.Identity, bias=conv_half[:, c, TAPS:],
                                         scale=conv_half[:, c, TAPS - 1:TAPS]).then_inc(conv_base, 1)
                if s - 2 in F_XX:
                    c = F_XX.index(s - 2)
                    act.wait_ge(conv_taps, r * (DC * (TAPS - 1)) + (c + 1) * (TAPS - 1))
                    nc.scalar.activation(delta2[:, par, c, :], y2[:, par, c, :], ACT.Tanh).then_inc(u_tanh, 1)
                if s == F_DBL_OUT:
                    act.wait_ge(pe_dbl, r + 1)
                    wait_past(act, c_stored, r * 16)
                    nc.scalar.activation(xdbl, misc_ps[0:DTC, :], ACT.Copy).then_inc(xdbl_ready, 1)
                if s == F_BT_OUT:
                    act.wait_ge(pe_bT, r + 1)
                    nc.scalar.activation(bT2[:, par], misc_ps[:, 0:TT * STATES].rearrange("p (t n) -> p t n", t=TT),
                                         ACT.Copy).then_inc(bT_ready, 1)
                if s - 2 in F_DT:
                    c = F_DT.index(s - 2)
                    act.wait_ge(dt_ready, r * DC + (c + 1))
                    nc.scalar.activation(du[:, c, :], delta2[:, par, c, :], ACT.Abs).then_inc(sp_abs, 1)
                    act.wait_ge(sp_abs, r * DC + (c + 1))
                    nc.scalar.activation(du[:, c, :], du[:, c, :], ACT.Exp, scale=-1.0).then_inc(sp_exp, 1)
                if s == F_LN:
                    for c in range(DC):
                        act.wait_ge(sp_lost, r * DC + (c + 1))
                        nc.scalar.activation(sp_w[c], sp_w[c], ACT.Ln).then_inc(sp_ln, 1)
                if s in F_DU:
                    t = F_DU.index(s)
                    act.wait_ge(pe_duT, r * TT + (t + 1))
                    wait_past(act, dB_ready, r * (STATES * TT) + (t + 1 - TT))
                    nc.scalar.activation(duT[:, t, :], misc_ps[:], ACT.Copy).then_inc(duT_ready, 1)

            def tail_step(r, s):
                if s in T_XT:
                    k = T_XT.index(s)
                    act.wait_ge(pe_tail_xT, r * KD + (k + 1))
                    nc.scalar.activation(xT[:, k, :], misc_ps[:], ACT.Copy).then_inc(tail_xT_ready, 1)
                if s - 1 in T_RES:
                    c = T_RES.index(s - 1)
                    act.wait_ge(pe_res, r * DC + (c + 1))
                    if c >= 2:
                        act.wait_ge(y_gated, r * DC + (c - 1))
                    nc.scalar.activation(gate[:, c % 2, :], misc_ps[:], ACT.Tanh).then_inc(v_tanh, 1)
                if s in T_X1T:
                    k = T_X1T.index(s)
                    act.wait_ge(pe_x1T, r * KD + (k + 1))
                    nc.scalar.activation(x1T_hi[:, k, :], misc_ps[:], ACT.Copy).then_inc(x1_hi, 1)

            def gelu_tiles(f, tiles):
                for i in tiles:
                    act.wait_ge(pe_half, f * HALVES + 2 * (i + 1))
                    act.wait_ge(ffn_lo, f * FFN_TILES + (HC + i - X32 + 1))
                    nc.scalar.activation(x32[:, i % X32, :], ffn_ps[(2 * HC + i) % 3][:], ACT.Gelu,
                                         scale=fs[:, 2 + i // HC, i % HC:i % HC + 1]).then_inc(gelu_x32, 1)

            def hi_tiles(f, tiles):
                for i in tiles:
                    act.wait_ge(gelu_x32, f * (2 * HC) + (i + 1))
                    if i == HC:
                        act.wait_ge(pe_half, f * HALVES + 2 * HC)
                    dst = hb_hi if i < HC else ha_hi
                    nc.scalar.activation(dst[:, i % HC, :], x32[:, i % X32, :], ACT.Copy).then_inc(ffn_hi, 1)

            def ffn_step(f, s):
                if A_L1 <= s < A_L1 + HC:
                    o = s - A_L1
                    act.wait_ge(pe_l1, f * (2 * HC) + (2 * o + 1))
                    if o >= 2:
                        act.wait_ge(l1_x32, f * HC + (o - 1))
                    nc.scalar.activation(gate[:, o % 2, :], ffn_ps[2 * o % 3][:], ACT.Tanh,
                                         scale=s1_half[:, o:o + 1]).then_inc(l1_tanh, 1)
                if A_L1 + A_HI <= s < A_L1 + A_HI + HC:
                    o = s - A_L1 - A_HI
                    act.wait_ge(l1_x32, f * HC + (o + 1))
                    nc.scalar.activation(ha_hi[:, o, :], x32[:, o % X32, :], ACT.Copy).then_inc(ffn_hi, 1)
                if s in GELU_AT:
                    gelu_tiles(f, GELU_AT[s])
                if s in HI_AT:
                    hi_tiles(f, HI_AT[s])

            def iteration(i, par):
                (scan, spar), (front, fpar), (tail, _), (end, _) = rows(i, par)
                for s in range(TILES):
                    for lead, step in ((EXP_LEAD, exp_tile), (SCALE_LEAD, scale_tile)):
                        if s + lead < TILES:
                            if scan is not None:
                                step(scan, spar, s + lead)
                        elif front is not None:
                            step(front, fpar, s + lead - TILES)
                    if (s + 4) % DC == 0:
                        n = (s + 4) // DC
                        if n < STATES:
                            if scan is not None:
                                load_c(scan, n)
                        elif front is not None:
                            load_c(front, 0)
                    if tail is not None:
                        tail_step(tail, s)
                    if front is not None:
                        front_step(front, fpar, s)
                    if tail is not None:
                        ffn_step(tail, s)
                    if end is not None:
                        ffn_step(end, s + TILES)
                    if isinstance(i, int) and i == 0:
                        if s in PREP_AT:
                            split_slot(PREP_AT[s])
                        if s - 1 in PREP_AT:
                            sum_low(PREP_AT[s - 1])

            iteration(-1, 1)
            iteration(0, 0)
            main_loop(act, iteration)

        @block.vector
        def _(dve):
            dve.wait_ge(const_loaded, 16 * CONST_LOADS)
            nc.vector.memset(ones[:], 1.0).then_inc(const_dve, 1)
            nc.vector.memset(eps[:], EPS).then_inc(const_dve, 1)
            nc.vector.memset(minus_half[:], -0.5).then_inc(const_dve, 1)
            nc.vector.tensor_scalar(conv_half[:], ch[:, :, 0:TAPS + 1], 0.5, None, ALU.mult).then_inc(const_dve, 1)
            nc.vector.tensor_scalar(inw[:, :, INNER:], inw[:, :, INNER:], 0.5, None, ALU.mult).then_inc(const_dve, 1)
            nc.vector.tensor_scalar(s1_half[:], fs[:, 0, :], 0.5, None, ALU.mult).then_inc(const_dve, 1)
            dve.wait_ge(const_exp, 1)
            nc.vector.tensor_scalar(a_neg[:], a_neg[:], -1.0, None, ALU.mult).then_inc(const_dve, 1)
            dve.wait_ge(const_dve, CONST_DVE)
            nc.vector.tensor_tensor(s12_half[:], s1_half[:], fs[:, 1, :], ALU.mult).then_inc(const_s12, 1)

            def split_low(k):
                dve.wait_ge(split_hi_done, k + 1)
                nc.vector.tensor_tensor(split_lo[:, k % SPLITS, :], raw[:, k % 2, :],
                                        split_hi[:, k % SPLITS, :].bitcast(F32), ALU.subtract
                                        ).then_inc(split_lo_done, 1)

            def scan_tile(r, s):
                dve.wait_ge(dA_ready, r * TILES + (s + 1))
                dve.wait_ge(pe_dBu, r * TILES + (s + 1))
                nc.vector.tensor_tensor_scan(scan_ps[:, s % 4], dA[:, s % 4], scan_ps[:, s % 4], 0.0,
                                             ALU.mult, ALU.add).then_inc(scan_done, 1)

            def c_pair(r, p):
                n = p // 2
                if p % 2 == 0:
                    dve.wait_ge(c_loaded[n % 2], r * (16 * STATES // 2) + 16 * (n // 2 + 1))
                wait_past(dve, y_added, r * PAIRS + (p - 1))
                dve.wait_ge(scan_done, r * TILES + (2 * p + 2))
                k = 2 * (p % 2)
                nc.vector.tensor_tensor(hC[:, p % 2], scan_ps[:, k:k + 2],
                                        c_rows[:, n % 2].unsqueeze(1).to_broadcast([P, 2, SEQ]),
                                        ALU.mult).then_inc(hC_done, 1)

            def front_step(r, par, s, tail, end):
                if s - 1 in F_XX:
                    c = F_XX.index(s - 1)
                    for back in range(1, TAPS):
                        if back == 1:
                            dve.wait_ge(conv_base, r * DC + (c + 1))
                        else:
                            dve.wait_ge(conv_taps, r * (DC * (TAPS - 1)) + (c * (TAPS - 1) + back - 1))
                        tap = TAPS - 1 - back
                        nc.vector.scalar_tensor_tensor(
                            out=y2[:, par, c, back:], in0=misc_ps[:, 0:SEQ - back], scalar=conv_half[:, c, tap:tap + 1],
                            in1=y2[:, par, c, back:], op0=ALU.mult, op1=ALU.add).then_inc(conv_taps, 1)
                if s - 2 in F_XX:
                    c = F_XX.index(s - 2)
                    dve.wait_ge(u_tanh, r * DC + (c + 1))
                    nc.vector.scalar_tensor_tensor(out=y2[:, par, c, :], in0=delta2[:, par, c, :], scalar=1.0,
                                                   in1=y2[:, par, c, :], op0=ALU.add, op1=ALU.mult
                                                   ).then_inc(u_ready, 1)
                if s - 1 in F_DT:
                    c = F_DT.index(s - 1)
                    dve.wait_ge(pe_dt, r * DC + (c + 1))
                    nc.vector.tensor_scalar(delta2[:, par, c, :], misc_ps[:], ch[:, c, C_DTB:C_DTB + 1], None,
                                            ALU.add).then_inc(dt_ready, 1)
                if s - 3 in F_DT:
                    c = F_DT.index(s - 3)
                    if c == 0 and end is not None:
                        dve.wait_ge(out_stored, end * 16 + 16)
                    if c == 2 and tail is not None:
                        dve.wait_ge(l1_x32, tail * HC + HC)
                    dve.wait_ge(sp_exp, r * DC + (c + 1))
                    nc.vector.tensor_scalar(sp_w[c], du[:, c, :], 1.0, None, ALU.add).then_inc(sp_plus, 1)
                    dve.wait_ge(sp_plus, r * DC + (c + 1))
                    nc.vector.scalar_tensor_tensor(out=du[:, c, :], in0=sp_w[c], scalar=1.0, in1=du[:, c, :],
                                                   op0=ALU.subtract, op1=ALU.subtract).then_inc(sp_lost, 1)
                if s - 4 in F_DT:
                    c = F_DT.index(s - 4)
                    dve.wait_ge(sp_lost, r * DC + (c + 1))
                    nc.vector.scalar_tensor_tensor(out=delta2[:, par, c, :], in0=delta2[:, par, c, :], scalar=0.0,
                                                   in1=du[:, c, :], op0=ALU.max, op1=ALU.subtract).then_inc(sp_max, 1)
                for c in range(DC):
                    if F_DELTA[c] == s:
                        dve.wait_ge(sp_max, r * DC + (c + 1))
                        dve.wait_ge(sp_ln, r * DC + (c + 1))
                        nc.vector.tensor_tensor(delta2[:, par, c, :], delta2[:, par, c, :], sp_w[c], ALU.add
                                                ).then_inc(delta_ready, 1)
                if s in F_Y:
                    c = F_Y.index(s)
                    dve.wait_ge(du_ready, r * DC + (c + 1))
                    nc.vector.tensor_scalar(y2[:, par, c, :], y2[:, par, c, :], ch[:, c, C_D:C_D + 1], None,
                                            ALU.mult).then_inc(y_init, 1)

            def statistics(which, src, r, ready):
                for t in range(TT):
                    dve.wait_ge(ready, r * 2 + (t // 2 + 1))
                    nc.vector.bn_stats(stats[:, which, t, :], src[:, t, :]).then_inc(ln_stats[which], 1)
                dve.wait_ge(ln_stats[which], r * TT + TT)
                nc.vector.tensor_copy(stats_seen[:, which:which + 1], stats[:, which, TT - 1, 0:1])
                for t in range(TT):
                    nc.vector.bn_aggr(mv[:, which, t, :], stats[:, which, t, :]).then_inc(ln_aggr[which], 1)

            def normalise(which, src, dst, r, done):
                dve.wait_ge(ln_rstd[which], r + 1)
                for t in range(TT):
                    nc.vector.tensor_scalar(dst[:, t, :], src[:, t, :], mv[:, which, t, 0:1],
                                            rstd[:, which, t:t + 1], ALU.subtract, ALU.mult).then_inc(done, 1)

            def tail_step(r, par, s):
                if s - 1 in T_RES:
                    c = T_RES.index(s - 1)
                    dve.wait_ge(v_tanh, r * DC + (c + 1))
                    nc.vector.scalar_tensor_tensor(out=gate[:, c % 2, :], in0=gate[:, c % 2, :], scalar=1.0,
                                                   in1=misc_ps[:], op0=ALU.add, op1=ALU.mult).then_inc(v_ready, 1)
                if s in T_ADD:
                    k = T_ADD.index(s)
                    dve.wait_ge(pe_out, r * TT + (2 * k + 2))
                    nc.vector.tensor_tensor(xt[:, 2 * k:2 * k + 2, :], misc_ps[:].rearrange("p (t d) -> p t d", t=2),
                                            xt[:, 2 * k:2 * k + 2, :], ALU.add).then_inc(z_ready, 1)
                if s == T_STATS:
                    statistics(0, xt, r, z_ready)
                if s == T_NORM:
                    normalise(0, xt, x1, r, x1_ready)
                if s in T_X1T:
                    k = T_X1T.index(s)
                    dve.wait_ge(x1_hi, r * KD + (k + 1))
                    nc.vector.tensor_tensor(x1T_lo[:, k, :], misc_ps[:], x1T_hi[:, k, :].bitcast(F32), ALU.subtract
                                            ).then_inc(x1_lo, 1)

            def l1_tile(f, o):
                dve.wait_ge(l1_tanh, f * HC + (o + 1))
                nc.vector.scalar_tensor_tensor(out=gate[:, o % 2, :], in0=gate[:, o % 2, :], scalar=1.0,
                                               in1=ffn_ps[2 * o % 3][:], op0=ALU.add, op1=ALU.mult
                                               ).then_inc(l1_gate, 1)
                dve.wait_ge(l1_gate, f * HC + (o + 1))
                dve.wait_ge(pe_l1, f * (2 * HC) + (2 * o + 2))
                if o >= X32:
                    dve.wait_ge(ffn_lo, f * FFN_TILES + (o - X32 + 1))
                nc.vector.scalar_tensor_tensor(out=x32[:, o % X32, :], in0=gate[:, o % 2, :],
                                               scalar=s12_half[:, o:o + 1], in1=ffn_ps[(2 * o + 1) % 3][:],
                                               op0=ALU.mult, op1=ALU.mult).then_inc(l1_x32, 1)

            def end_step(f, s):
                if s in E_SCALE:
                    k = E_SCALE.index(s)
                    dve.wait_ge(pe_w3, f * TT + 2 * (k + 1))
                    nc.vector.tensor_tensor(out_st[:, 2 * k:2 * k + 2, :],
                                            ffn_ps[(4 * HC + k) % 3][:].rearrange("p (t d) -> p t d", t=2),
                                            w3s[:].unsqueeze(1).to_broadcast([P, 2, DIM]), ALU.mult
                                            ).then_inc(w3_scaled, 1)
                if s in E_ADD:
                    k = E_ADD.index(s)
                    dve.wait_ge(w3_scaled, f * 2 + (k + 1))
                    nc.vector.tensor_tensor(out_st[:, 2 * k:2 * k + 2, :], out_st[:, 2 * k:2 * k + 2, :],
                                            x1[:, 2 * k:2 * k + 2, :], ALU.add).then_inc(z2_ready, 1)
                if s == E_STATS:
                    statistics(1, out_st, f, z2_ready)
                if s == E_NORM:
                    normalise(1, out_st, out_st, f, out_ready)

            def iteration(i, par):
                (scan, _), (front, fpar), (tail, tpar), (end, _) = rows(i, par)
                for s in range(TILES):
                    if scan is not None:
                        scan_tile(scan, s)
                        if s % 2:
                            c_pair(scan, s // 2)
                    if end is not None:
                        end_step(end, s)
                    if tail is not None:
                        tail_step(tail, tpar, s)
                    if front is not None:
                        front_step(front, fpar, s, tail, end)
                    if tail is not None and A_L1 <= s < A_L1 + HC:
                        l1_tile(tail, s - A_L1)
                    if isinstance(i, int) and i == 0 and s in PREP_AT:
                        split_low(PREP_AT[s])

            iteration(-1, 1)
            iteration(0, 0)
            dve.wait_ge(split_sum_done, SLOTS)
            nc.vector.tensor_reduce(low_sum[:], low_sums[:], mybir.AxisListType.X, ALU.add).then_inc(low_summed, 1)
            dve.wait_ge(low_total, 1)
            nc.vector.tensor_copy(low_flag[:], ffn_ps[0][0:1, 0:1]).then_inc(flag_ready, 1)
            main_loop(dve, iteration)

        @block.gpsimd
        def _(pool):
            pool.wait_ge(const_dve, CONST_DVE)

            def y_pair(r, par, p):
                pool.wait_ge(hC_done, r * PAIRS + (p + 1))
                if p == 0:
                    pool.wait_ge(y_init, r * DC + DC)
                if p >= 2:
                    pool.wait_ge(y_added, r * PAIRS + (p - 1))
                c = 2 * (p % 2)
                nc.gpsimd.tensor_tensor(y2[:, par, c:c + 2, :], y2[:, par, c:c + 2, :], hC[:, p % 2], ALU.add
                                        ).then_inc(y_added, 1)

            def gate_tile(r, par, c):
                if c == 0:
                    pool.wait_ge(y_added, r * PAIRS + PAIRS)
                pool.wait_ge(v_ready, r * DC + (c + 1))
                nc.gpsimd.tensor_tensor(y2[:, par, c, :], y2[:, par, c, :], gate[:, c % 2, :], ALU.mult
                                        ).then_inc(y_gated, 1)

            def du_tile(r, par, c):
                pool.wait_ge(delta_ready, r * DC + (c + 1))
                nc.gpsimd.tensor_tensor(du[:, c, :], y2[:, par, c, :], delta2[:, par, c, :], ALU.mult
                                        ).then_inc(du_ready, 1)

            def rstd_of(which, r):
                pool.wait_ge(ln_aggr[which], r * TT + TT)
                nc.gpsimd.tensor_tensor(var_eps[:, which], mv[:, which, :, 1], eps[:], ALU.add
                                        ).then_inc(ln_eps[which], 1)
                pool.wait_ge(ln_eps[which], r + 1)
                nc.gpsimd.tensor_tensor(rstd[:, which], var_eps[:, which], minus_half[:], ALU.pow
                                        ).then_inc(ln_rstd[which], 1)

            def low_tile(f, i):
                pool.wait_ge(ffn_hi, f * FFN_TILES + (i + 1))
                hi, lo = (hb_hi, hb_lo) if HC <= i < 2 * HC else (ha_hi, ha_lo)
                nc.gpsimd.tensor_tensor(lo[:, i % HC, :], x32[:, i % X32, :], hi[:, i % HC, :].bitcast(F32),
                                        ALU.subtract).then_inc(ffn_lo, 1)

            def ffn_step(f, s):
                if A_L1 + A_LO <= s < A_L1 + A_LO + HC:
                    low_tile(f, s - A_L1 - A_LO)
                for i in HI_AT.get(s - LO_AFTER, ()):
                    low_tile(f, HC + i)

            def iteration(i, par):
                (scan, spar), (front, fpar), (tail, tpar), (end, _) = rows(i, par)
                for s in range(TILES):
                    if scan is not None and s % 2:
                        y_pair(scan, spar, s // 2)
                    if tail is not None:
                        if s - 2 in T_RES:
                            gate_tile(tail, tpar, T_RES.index(s - 2))
                        if s == T_STATS:
                            rstd_of(0, tail)
                        ffn_step(tail, s)
                    if end is not None:
                        if s == E_STATS:
                            rstd_of(1, end)
                        ffn_step(end, s + TILES)
                    if front is not None and s in F_DELTA_U:
                        du_tile(front, fpar, F_DELTA_U.index(s))

            iteration(-1, 1)
            iteration(0, 0)
            main_loop(pool, iteration)


def kernel(L0_attn_x, L0_attn_in_w, L0_attn_conv_w, L0_attn_conv_b, L0_attn_xproj_w, L0_attn_dt_w, L0_attn_dt_b,
           L0_attn_A_log, L0_attn_D, L0_attn_out_w, L0_ffn_w1_w, L0_ffn_w1_s, L0_ffn_w2_w, L0_ffn_w2_s,
           L0_ffn_h1_w, L0_ffn_h1_s, L0_ffn_h2_w, L0_ffn_h2_s, L0_ffn_w3_w, L0_ffn_w3_s):
    import numpy as np
    import concourse.bacc as bacc
    from concourse.bass_utils import run_bass_kernel_spmd

    def ktiles(wT):
        return wT.reshape(-1, P, wT.shape[1]).transpose(1, 0, 2)

    def channels(a):
        return a.reshape(-1, P, a.shape[1]).transpose(1, 0, 2)

    A = np.asarray
    chan = np.concatenate([channels(A(L0_attn_conv_w)[:, 0, :])]
                          + [channels(A(a)[:, None]) for a in (L0_attn_conv_b, L0_attn_D, L0_attn_dt_b)]
                          + [channels(A(L0_attn_A_log))], axis=2)
    w1, w2, h1, h2, w3 = (ktiles(A(w).T) for w in (L0_ffn_w1_w, L0_ffn_w2_w, L0_ffn_h1_w, L0_ffn_h2_w, L0_ffn_w3_w))
    slots = []
    for s in range(L1_SLOTS):
        tiles = [w[:, :, o * P:(o + 1) * P] for o in (2 * s, 2 * s + 1) for w in (w1, w2)]
        slots.append(np.concatenate(tiles, axis=1).reshape(P, SLOT_COLS))
    for w in (h1, h2):
        slots += [w[:, :, o * P:(o + 1) * P].reshape(P, SLOT_COLS) for o in range(HC)]
    slots += [w3[:, 4 * h:4 * h + 4, :].reshape(P, SLOT_COLS) for h in range(W3_SLOTS)]
    scales = np.concatenate([channels(A(s)[:, None]).transpose(0, 2, 1)
                             for s in (L0_ffn_w1_s, L0_ffn_w2_s, L0_ffn_h1_s, L0_ffn_h2_s)], axis=1)
    arrays = {
        "x_tok": A(L0_attn_x).reshape(BATCH, TT, P, DIM).transpose(0, 2, 1, 3),
        "in_wT": ktiles(A(L0_attn_in_w).T),
        "chan": chan,
        "xproj_wT": ktiles(A(L0_attn_xproj_w).T)[:, :, np.r_[0:RANK, RANK + STATES:RANK + 2 * STATES,
                                                             RANK:RANK + STATES]],
        "dt_wT": A(L0_attn_dt_w).T,
        "out_wT": ktiles(A(L0_attn_out_w).T),
        "ffn_w": np.stack(slots),
        "ffn_s": scales,
        "w3_s": A(L0_ffn_w3_s),
        "identity": np.eye(P, dtype=np.float32),
    }
    arrays = {n: np.ascontiguousarray(a) for n, a in arrays.items()}
    nc = bacc.Bacc("TRN2", target_bir_lowering=False, num_devices=1)
    args = [nc.dram_tensor(n, list(a.shape), mybir.dt.from_np(a.dtype), kind="ExternalInput").ap()
            for n, a in arrays.items()]
    out = nc.dram_tensor("out_tok", [BATCH, P, TT, DIM], F32, kind="ExternalOutput").ap()
    build(nc, *args, out)
    r = run_bass_kernel_spmd(nc, [arrays], core_ids=[0])
    return r.results[0]["out_tok"].transpose(0, 2, 1, 3).reshape(BATCH, SEQ, DIM)
```

```python
from contextlib import ExitStack

import concourse.bass as bass
from concourse import mybir

F32 = mybir.dt.float32
F32R = mybir.dt.float32r
I32 = mybir.dt.int32
ALU = mybir.AluOpType
ACT = mybir.ActivationFunctionType

P = 128
BATCH, SEQ, DIM = 16, 512, 256
INNER, STATES, RANK, TAPS, HIDDEN = 512, 16, 16, 4, 1024
KD = DIM // P
DC = INNER // P
HC = HIDDEN // P
TT = SEQ // P
TILES = STATES * DC
PAIRS = TILES // 2
DTC = RANK + STATES
EPS = 1e-5

C_CONVB, C_D, C_DTB, C_ALOG = TAPS, TAPS + 1, TAPS + 2, TAPS + 3
CHAN = TAPS + 3 + STATES

L1_SLOTS, W3_SLOTS = HC // 2, 2
SLOTS = L1_SLOTS + 2 * HC + W3_SLOTS
SLOT_COLS = HC * P
ENTRY_COLS = SLOT_COLS // 2
RING = 4
HALVES = 4 * HC
QUARTERS = 2 * W3_SLOTS

T_XT = (61, 62)
T_RES, T_GATE = (0, 3, 6, 8), (2, 5, 7, 10)
T_OUT, T_ADD, T_STATS, T_NORM, T_X1T = (12, 13, 14, 15), (15, 17), (16, 18), 19, (20, 21)
E_W3, E_SCALE, E_ADD, E_STATS, E_NORM = (11, 12, 13, 14), (15, 16), (16, 17), (19, 20), 22
A_L1 = 22
A_HI, A_LO = 2, 3
HALF_AT = [33, 34, 35, 36, 37, 38, 40, 41, 42, 43, 44, 45, 47, 48, 49, 50,
           54, 55, 56, 57, 58, 59, 61, 62, 63, 64, 65, 66, 68, 69, 70, 71]
GELU_AT = {39: (0, 1), 40: (2,), 46: (3, 4), 47: (5,), 51: (6, 7), 52: (),
           60: (8, 9), 61: (10,), 67: (11, 12), 68: (13,), 72: (14, 15), 73: ()}
HI_AT = {40: (0,), 41: (1,), 42: (2,), 47: (3,), 48: (4,), 49: (5,), 52: (6, 7),
         61: (8,), 62: (9,), 63: (10,), 68: (11,), 69: (12,), 70: (13,), 73: (14, 15)}
LO_AFTER = 1
F_XT, F_XX, F_DBL, F_DBL_OUT, F_BT, F_BT_OUT = (26, 28), (30, 32, 34, 36), 39, 40, 45, 46
F_DT, F_EXP, F_PLUS, F_MAX, F_LN = (41, 42, 43, 44), (43, 44, 45, 48), (44, 45, 46, 49), (45, 46, 47, 50), 51
F_DELTA, F_DELTA_U, F_Y, F_DU = (54, 54, 55, 55), (54, 54, 55, 55), (57, 58, 59, 60), (56, 57, 58, 59)
B_LEAD, SCALE_LEAD = 3, 7
EXP_LEAD, DA_RING = 4, 8
NO_EXP = {s % TILES for s in GELU_AT}
EXP_COUNT = [0 if s in NO_EXP else 2 if {(s + 1) % TILES, (s + 2) % TILES} & NO_EXP else 1 for s in range(TILES)]
EXP_FIRST = EXP_LEAD + len({0, 1} & NO_EXP)
EXP_AT = [(EXP_FIRST + sum(EXP_COUNT[:s]), EXP_COUNT[s]) for s in range(TILES)]
PREP_AT = {2 * k: k for k in range(SLOTS)}
X32 = 4
SPLITS = 4


def build(nc, x, in_wT, chan, xproj_wT, dt_wT, out_wT, ffn_w, ffn_s, w3_s, ident_in, out):
    c_dram = nc.dram_tensor("c_rows", [BATCH, STATES, SEQ], F32, kind="Internal").ap()
    w_dram = nc.dram_tensor("split_weights", [2, SLOTS, P, SLOT_COLS], F32, kind="Internal").ap()

    with ExitStack() as ctx:
        def sb(name, shape, dt=F32):
            return ctx.enter_context(nc.sbuf_tensor(name, shape, dt))

        def sem(name):
            return ctx.enter_context(nc.semaphore(name))

        ident = sb("ident", [P, P])
        inw = sb("inw", [P, KD, 2 * INNER])
        outw = sb("outw", [P, DC, DIM])
        xprojw = sb("xprojw", [P, DC, DTC + STATES])
        dtw = sb("dtw", [RANK, INNER])
        ch = sb("ch", [P, DC, CHAN])
        fs = sb("fs", [P, 4, HC])
        w3s = sb("w3s", [P, DIM])
        conv_half = sb("conv_half", [P, DC, TAPS + 1])
        a_neg = sb("a_neg", [P, DC, STATES])
        s1_half = sb("s1_half", [P, HC])
        s12_half = sb("s12_half", [P, HC])
        minus_half = sb("minus_half", [P, TT])
        eps = sb("eps", [P, TT])
        ones = sb("ones", [P, 1])
        low_sums = sb("low_sums", [P, SLOTS])
        low_sum = sb("low_sum", [P, 1])
        low_flag = sb("low_flag", [1, 1])
        xt = sb("xt", [P, TT, DIM])
        y2 = sb("y2", [P, 2, DC, SEQ])
        delta2 = sb("delta2", [P, 2, DC, SEQ])
        bT2 = sb("bT2", [P, 2, TT, STATES])
        du = sb("du", [P, DC, SEQ])
        duT = sb("duT", [P, TT, INNER])
        c_rows = sb("c_rows_sb", [P, 2, SEQ])
        dB = sb("dB", [P, 2, TT, INNER])
        dA = sb("dA", [P, DA_RING, SEQ])
        hC = sb("hC", [P, 2, 2, SEQ])
        ring = sb("ring", [P, RING, ENTRY_COLS], F32R)
        x1 = sb("x1", [P, TT, DIM])
        ha_hi = sb("ha_hi", [P, HC, SEQ], F32R)
        ha_lo = sb("ha_lo", [P, HC, SEQ], F32R)
        hb_hi = sb("hb_hi", [P, HC, SEQ], F32R)
        hb_lo = sb("hb_lo", [P, HC, SEQ], F32R)
        gate = sb("gate", [P, 2, SEQ])
        x32 = sb("x32", [P, X32, SEQ])
        out_st = sb("out_st", [P, TT, DIM])
        stats = sb("stats", [P, 2, TT, 6])
        stats_seen = sb("stats_seen", [P, 2])
        mv = sb("mv", [P, 2, TT, 2])
        var_eps = sb("var_eps", [P, 2, TT])
        rstd = sb("rstd", [P, 2, TT])

        xT = out_st[:].rearrange("p (k t) d -> p k (t d)", k=KD)
        xdbl = xT[0:DTC + STATES, 1, :]
        x1T_hi, x1T_lo = hb_hi[:, 0:KD, :], hb_lo[:, 0:KD, :]
        out_halves = out_st[:].rearrange("p (a t) d -> p a (t d)", a=2)
        sp_w = [out_halves[:, 0], gate[:, 0, :], gate[:, 1, :], out_halves[:, 1]]
        raw = x32[:].rearrange("p (s a) l -> p s (a l)", s=2)
        split_hi = ha_hi[:].rearrange("p (s a) l -> p s (a l)", s=SPLITS)
        split_lo = ha_lo[:].rearrange("p (s a) l -> p s (a l)", s=SPLITS)

        scan_ps = ctx.enter_context(nc.psum_tensor("scan_ps", [P, 4, SEQ], F32))
        ffn_ps = [ctx.enter_context(nc.psum_tensor(f"ffn_ps{i}", [P, SEQ], F32)) for i in range(3)]
        misc_ps = ctx.enter_context(nc.psum_tensor("misc_ps", [P, SEQ], F32))

        out_ps = [misc_ps, ffn_ps[1]]

        const_loaded = sem("const_loaded")
        raw_loaded = [sem(f"raw_loaded{i}") for i in range(2)]
        split_stored = [sem(f"split_stored{i}") for i in range(SPLITS)]
        xf_loaded = sem("xf_loaded")
        xr_loaded = sem("xr_loaded")
        c_stored = sem("c_stored")
        c_loaded = [sem(f"c_loaded{i}") for i in range(2)]
        ring_loaded = [sem(f"ring_loaded{i}") for i in range(RING)]
        out_stored = sem("out_stored")
        const_dve, const_exp, const_s12 = sem("const_dve"), sem("const_exp"), sem("const_s12")
        split_hi_done, split_lo_done = sem("split_hi_done"), sem("split_lo_done")
        split_sum_done, low_summed = sem("split_sum_done"), sem("low_summed")
        low_total, flag_ready = sem("low_total"), sem("flag_ready")
        pe_xT, pe_xx, pe_dbl, pe_bT = sem("pe_xT"), sem("pe_xx"), sem("pe_dbl"), sem("pe_bT")
        pe_dt, pe_duT, pe_dBu = sem("pe_dt"), sem("pe_duT"), sem("pe_dBu")
        pe_tail_xT, pe_res, pe_out, pe_x1T = sem("pe_tail_xT"), sem("pe_res"), sem("pe_out"), sem("pe_x1T")
        pe_l1, pe_half, pe_w3, pe_quarter = sem("pe_l1"), sem("pe_half"), sem("pe_w3"), sem("pe_quarter")
        xT_ready, conv_base, conv_taps = sem("xT_ready"), sem("conv_base"), sem("conv_taps")
        u_tanh, u_ready, xdbl_ready, bT_ready = sem("u_tanh"), sem("u_ready"), sem("xdbl_ready"), sem("bT_ready")
        dt_ready, sp_abs, sp_exp, sp_plus = sem("dt_ready"), sem("sp_abs"), sem("sp_exp"), sem("sp_plus")
        sp_lost, sp_ln, sp_max = sem("sp_lost"), sem("sp_ln"), sem("sp_max")
        delta_ready, du_ready, y_init = sem("delta_ready"), sem("du_ready"), sem("y_init")
        duT_ready = sem("duT_ready")
        dB_ready, dA_ready, scan_done = sem("dB_ready"), sem("dA_ready"), sem("scan_done")
        hC_done, y_added = sem("hC_done"), sem("y_added")
        tail_xT_ready, v_tanh, v_ready = sem("tail_xT_ready"), sem("v_tanh"), sem("v_ready")
        y_gated, z_ready = sem("y_gated"), sem("z_ready")
        x1_ready, x1_hi, x1_lo = sem("x1_ready"), sem("x1_hi"), sem("x1_lo")
        ln_stats = [sem(f"ln_stats{i}") for i in range(2)]
        ln_aggr = [sem(f"ln_aggr{i}") for i in range(2)]
        ln_eps = [sem(f"ln_eps{i}") for i in range(2)]
        ln_rstd = [sem(f"ln_rstd{i}") for i in range(2)]
        l1_tanh, l1_gate, l1_x32 = sem("l1_tanh"), sem("l1_gate"), sem("l1_x32")
        gelu_x32, ffn_hi, ffn_lo = sem("gelu_x32"), sem("ffn_hi"), sem("ffn_lo")
        w3_scaled, z2_ready, out_ready = sem("w3_scaled"), sem("z2_ready"), sem("out_ready")

        block = ctx.enter_context(nc.Block())

        CONST_LOADS, CONST_DVE = 8, 7
        FFN_TILES = 3 * HC

        def wait_past(eng, semaphore, value):
            if not (isinstance(value, int) and value <= 0):
                eng.wait_ge(semaphore, value)

        def rows(i, par):
            def row(k):
                if isinstance(i, int) and not 0 <= i + k < BATCH:
                    return None, None
                return i + k, (par + k) % 2
            return row(0), row(1), row(-1), row(-2)

        def main_loop(eng, iteration, *args):
            iteration(1, 1, *args)
            with eng.Fori(0, (BATCH - 4) // 2) as j:
                for h in range(2):
                    iteration(2 * j + (2 + h), h, *args)
            for i in range(BATCH - 2, BATCH + 2):
                iteration(i, i % 2, *args)

        def ring_entries(parts):
            halves = HC * parts
            w3 = halves + HALVES * parts
            return halves, w3, w3 + (QUARTERS if parts == 1 else TT * QUARTERS * parts)

        @block.sync
        def _(sp):
            for dst, src in ((ident[:], ident_in), (inw[:], in_wT), (ch[:], chan), (xprojw[:], xproj_wT),
                             (dtw[:], dt_wT), (outw[:], out_wT), (fs[:], ffn_s),
                             (w3s[:], w3_s.partition_broadcast(P))):
                sp.dma_start(dst, src).then_inc(const_loaded, 16)

            def load_front(r):
                sp.dma_start(xt[:], x[r]).then_inc(xf_loaded, 16)

            def load_tail(i, front):
                if front is not None:
                    sp.wait_ge(pe_xT, front * KD + KD)
                else:
                    sp.wait_ge(x1_ready, i * TT)
                sp.dma_start(xt[:], x[i]).then_inc(xr_loaded, 16)

            def store_c(r):
                sp.wait_ge(xdbl_ready, r + 1)
                sp.dma_start(c_dram[r], xdbl[RANK:DTC, :]).then_inc(c_stored, 16)

            def store_parts(k):
                sp.wait_ge(split_lo_done, k + 1)
                for p, part in enumerate((split_hi, split_lo)):
                    sp.dma_start(w_dram[p, k], part[:, k % SPLITS, :].bitcast(F32)
                                 ).then_inc(split_stored[k % SPLITS], 16)

            def load_weights(f, entries, parts):
                first_half, first_w3, total = ring_entries(parts)
                for e in entries:
                    used = e - RING
                    if used < 0:
                        wait_past(sp, pe_w3, f * TT)
                    elif used < first_half:
                        sp.wait_ge(pe_l1, f * (2 * HC) + 2 * (used // parts + 1))
                    elif used < first_w3:
                        sp.wait_ge(pe_half, f * HALVES + ((used - first_half) // parts + 1))
                    else:
                        t, q = divmod((used - first_w3) // parts, QUARTERS)
                        if q == QUARTERS - 1:
                            sp.wait_ge(pe_w3, f * TT + (t + 1))
                        else:
                            sp.wait_ge(pe_quarter, f * (TT * (QUARTERS - 1)) + (t * (QUARTERS - 1) + q + 1))
                    if e < first_half:
                        half, part = divmod(e, parts)
                    elif e < first_w3:
                        half, part = divmod(e - first_half, parts)
                        half += HC
                    else:
                        half, part = divmod((e - first_w3) % (QUARTERS * parts), parts)
                        half += HC + HALVES
                    sp.dma_start(ring[:, e % RING, :].bitcast(F32),
                                 w_dram[part, half // 2][:, (half % 2) * ENTRY_COLS:(half % 2 + 1) * ENTRY_COLS]
                                 ).then_inc(ring_loaded[e % RING], 16)

            load_front(0)
            for k in range(2):
                sp.dma_start(raw[:, k, :], ffn_w[k]).then_inc(raw_loaded[k], 16)
            store_c(0)
            sp.wait_ge(pe_xT, KD)
            load_front(1)
            for slot, k in PREP_AT.items():
                if slot == F_XT[-1] + F_XT[-1] % 2 + 2:
                    load_tail(0, 1)
                if slot == F_DBL_OUT + F_DBL_OUT % 2:
                    store_c(1)
                store_parts(k)
                if k + 2 < SLOTS:
                    sp.wait_ge(split_sum_done, k + 1)
                    sp.dma_start(raw[:, k % 2, :], ffn_w[k + 2]).then_inc(raw_loaded[k % 2], 16)
            for n in range(SPLITS):
                sp.wait_ge(split_stored[n], 32 * len(range(n, SLOTS, SPLITS)))
            sp.wait_ge(flag_ready, 1)
            general = sp.value_load(low_flag[0:1, 0:1].bitcast(I32))

            def iteration(i, par, parts):
                (_, _), (front, _), (tail, _), (end, _) = rows(i, par)
                first_half, first_w3, total = ring_entries(parts)
                if end is not None:
                    load_weights(end, range(first_w3, total), parts)
                if tail is not None:
                    load_weights(tail, range(RING), parts)
                    if front is not None:
                        sp.wait_ge(x1_ready, tail * TT + TT)
                        load_front(front)
                if end is not None:
                    sp.wait_ge(out_ready, end * TT + TT)
                    sp.dma_start(out[end], out_st[:]).then_inc(out_stored, 16)
                if tail is not None:
                    load_weights(tail, range(RING, first_half), parts)
                    if not (isinstance(i, int) and i >= BATCH):
                        load_tail(i, front)
                    mid = first_half + parts * sum(h < F_DBL_OUT for h in HALF_AT) + RING
                    load_weights(tail, range(first_half, mid), parts)
                    if front is not None:
                        store_c(front)
                    load_weights(tail, range(mid, first_w3), parts)

            with sp.If(general > 0):
                main_loop(sp, iteration, 2)
            with sp.Else():
                main_loop(sp, iteration, 1)
            sp.wait_ge(out_stored, 16 * BATCH)
            sp.wait_ge(c_stored, 16 * BATCH)

        @block.tensor
        def _(pe):
            pe.wait_ge(const_loaded, 16 * CONST_LOADS)
            pe.wait_ge(const_dve, CONST_DVE)

            def transposes(dst, src, n):
                for j in range(n):
                    mm = nc.tensor.transpose(dst[:, j * P:(j + 1) * P], src(j), ident[:])
                return mm

            def in_proj(col):
                for k in range(KD):
                    mm = nc.tensor.matmul(misc_ps[:], inw[:, k, col * P:(col + 1) * P], xT[:, k, :],
                                          start=(k == 0), stop=(k == KD - 1))
                return mm

            def b_tile(r, s):
                n, c = divmod(s, DC)
                if c == 0:
                    pe.wait_ge(dB_ready, r * (STATES * TT) + (n + 1) * TT)
                wait_past(pe, hC_done, r * TILES + (s - 3))
                transposes(scan_ps[:, s % 4], lambda t: dB[:, n % 2, t, c * P:(c + 1) * P], TT
                           ).then_inc(pe_dBu, 1)

            def front_step(i, r, par, s, tail):
                if s in F_XT:
                    k = F_XT.index(s)
                    if k:
                        pe.wait_ge(xT_ready, r * KD + k)
                    else:
                        pe.wait_ge(xf_loaded, r * 16 + 16)
                        if tail is not None:
                            pe.wait_ge(x1_lo, tail * KD + KD)
                        else:
                            wait_past(pe, duT_ready, i * TT + TT)
                    transposes(misc_ps, lambda t: xt[:, t, k * P:(k + 1) * P], TT).then_inc(pe_xT, 1)
                if s in F_XX:
                    c = F_XX.index(s)
                    if c:
                        pe.wait_ge(conv_taps, r * (DC * (TAPS - 1)) + c * (TAPS - 1))
                    else:
                        pe.wait_ge(xT_ready, r * KD + KD)
                    in_proj(c).then_inc(pe_xx, 1)
                if s == F_DBL:
                    pe.wait_ge(u_ready, r * DC + DC)
                    for c in range(DC):
                        mm = nc.tensor.matmul(misc_ps[0:DTC + STATES, :], xprojw[:, c, :], y2[:, par, c, :],
                                              start=(c == 0), stop=(c == DC - 1))
                    mm.then_inc(pe_dbl, 1)
                if s == F_BT:
                    pe.wait_ge(dt_ready, r * DC + DC)
                    for t in range(TT):
                        mm = nc.tensor.matmul(misc_ps[:, t * STATES:(t + 1) * STATES], xdbl[DTC:, t * P:(t + 1) * P],
                                              ident[DTC:DTC + STATES, DTC:DTC + STATES], start=True, stop=True)
                    mm.then_inc(pe_bT, 1)
                if s in F_DT:
                    c = F_DT.index(s)
                    if c:
                        pe.wait_ge(dt_ready, r * DC + c)
                    else:
                        pe.wait_ge(xdbl_ready, r + 1)
                    nc.tensor.matmul(misc_ps[:], dtw[:, c * P:(c + 1) * P], xdbl[0:RANK, :],
                                     start=True, stop=True).then_inc(pe_dt, 1)
                if s in F_DU:
                    t = F_DU.index(s)
                    if t:
                        pe.wait_ge(duT_ready, r * TT + t)
                    else:
                        pe.wait_ge(du_ready, r * DC + DC)
                        pe.wait_ge(bT_ready, r + 1)
                    transposes(misc_ps, lambda c: du[:, c, t * P:(t + 1) * P], DC).then_inc(pe_duT, 1)

            def tail_xT(r, s):
                if s in T_XT:
                    k = T_XT.index(s)
                    if k:
                        pe.wait_ge(tail_xT_ready, r * KD + k)
                    elif isinstance(r, int) and r == BATCH - 1:
                        pe.wait_ge(x1_lo, r * KD)
                    else:
                        pe.wait_ge(duT_ready, r * TT + 2 * TT)
                    if not k:
                        pe.wait_ge(xr_loaded, r * 16 + 16)
                    transposes(misc_ps, lambda t: xt[:, t, k * P:(k + 1) * P], TT).then_inc(pe_tail_xT, 1)

            def tail_step(r, par, s):
                if s in T_RES:
                    c = T_RES.index(s)
                    if c:
                        pe.wait_ge(v_ready, r * DC + c)
                    else:
                        pe.wait_ge(tail_xT_ready, r * KD + KD)
                    in_proj(DC + c).then_inc(pe_res, 1)
                if s in T_OUT:
                    t = T_OUT.index(s)
                    if t == 0:
                        pe.wait_ge(y_gated, r * DC + DC)
                    for c in range(DC):
                        mm = nc.tensor.matmul(out_ps[t // 2][:, (t % 2) * DIM:(t % 2 + 1) * DIM],
                                              y2[:, par, c, t * P:(t + 1) * P], outw[:, c, :],
                                              start=(c == 0), stop=(c == DC - 1))
                    mm.then_inc(pe_out, 1)
                if s in T_X1T:
                    k = T_X1T.index(s)
                    if k:
                        pe.wait_ge(x1_lo, r * KD + k)
                    else:
                        pe.wait_ge(x1_ready, r * TT + TT)
                    transposes(misc_ps, lambda t: x1[:, t, k * P:(k + 1) * P], TT).then_inc(pe_x1T, 1)

            def wait_entry(f, e, parts):
                per_row = ring_entries(parts)[2] // RING
                pe.wait_ge(ring_loaded[e % RING], f * (16 * per_row) + 16 * (e // RING + 1))

            def products(dst, steps, first, last):
                for n, (w, a) in enumerate(steps):
                    mm = nc.tensor.matmul(dst, w, a, start=(first and n == 0), stop=(last and n == len(steps) - 1))
                return mm

            def l1_tile(f, o, parts):
                if o == 0:
                    pe.wait_ge(x1_lo, f * KD + KD)
                for p in range(parts):
                    wait_entry(f, o * parts + p, parts)
                for q in range(2):
                    job = 2 * o + q
                    if job >= 3:
                        prev = job - 3
                        pe.wait_ge(l1_x32 if prev % 2 else l1_gate, f * HC + (prev // 2 + 1))
                    steps = [(ring[:, (o * parts + p) % RING, (q * KD + k) * P:(q * KD + k + 1) * P], a[:, k, :])
                             for p in range(parts) for k in range(KD) for a in (x1T_hi, x1T_lo)]
                    products(ffn_ps[job % 3][:], steps, True, True).then_inc(pe_l1, 1)

            def half_tile(f, m, parts):
                i, kh = divmod(m, 2)
                src = (ha_hi, ha_lo) if i < HC else (hb_hi, hb_lo)
                job = 2 * HC + i
                if i % HC == 0:
                    pe.wait_ge(ffn_lo, f * FFN_TILES + (i // HC * HC + (kh + 1) * HC // 2))
                if kh == 0:
                    prev = job - 3
                    if prev < 2 * HC:
                        pe.wait_ge(l1_x32 if prev % 2 else l1_gate, f * HC + (prev // 2 + 1))
                    else:
                        pe.wait_ge(gelu_x32, f * (2 * HC) + (prev - 2 * HC + 1))
                first_half = ring_entries(parts)[0]
                steps = []
                for p in range(parts):
                    e = first_half + m * parts + p
                    wait_entry(f, e, parts)
                    steps += [(ring[:, e % RING, k * P:(k + 1) * P], a[:, kh * HC // 2 + k, :])
                              for k in range(HC // 2) for a in src]
                products(ffn_ps[job % 3][:], steps, kh == 0, kh == 1).then_inc(pe_half, 1)

            def w3_tile(f, t, parts):
                job = 4 * HC + t // 2
                first_w3 = ring_entries(parts)[1]
                if t % 2 == 0:
                    pe.wait_ge(gelu_x32, f * (2 * HC) + (job - 3 - 2 * HC + 1))
                for q in range(QUARTERS):
                    steps = []
                    if t == 0:
                        pe.wait_ge(ffn_lo, f * FFN_TILES + (2 * HC + 2 * q + 2))
                    for p in range(parts):
                        e = first_w3 + (q if parts == 1 else (t * QUARTERS + q) * parts + p)
                        if parts > 1 or t == 0:
                            wait_entry(f, e, parts)
                        steps += [(a[:, 2 * q + k, t * P:(t + 1) * P], ring[:, e % RING, k * DIM:(k + 1) * DIM])
                                  for k in range(2) for a in (ha_hi, ha_lo)]
                    mm = products(ffn_ps[job % 3][:, (t % 2) * DIM:(t % 2 + 1) * DIM], steps, q == 0,
                                  q == QUARTERS - 1)
                    if q == QUARTERS - 1:
                        mm.then_inc(pe_w3, 1)
                    elif parts > 1:
                        mm.then_inc(pe_quarter, 1)

            def iteration(i, par, parts):
                (scan, _), (front, fpar), (tail, tpar), (end, _) = rows(i, par)
                for s in range(TILES):
                    if s + B_LEAD < TILES:
                        if scan is not None:
                            b_tile(scan, s + B_LEAD)
                    elif front is not None:
                        b_tile(front, s + B_LEAD - TILES)
                    if end is not None and s in E_W3:
                        w3_tile(end, E_W3.index(s), parts)
                    if tail is not None:
                        tail_step(tail, tpar, s)
                    if front is not None:
                        front_step(i, front, fpar, s, tail)
                    if scan is not None:
                        tail_xT(scan, s)
                    if end is not None:
                        if s + TILES in HALF_AT:
                            half_tile(end, HALF_AT.index(s + TILES), parts)
                    if tail is not None:
                        if A_L1 <= s < A_L1 + HC:
                            l1_tile(tail, s - A_L1, parts)
                        if s in HALF_AT:
                            half_tile(tail, HALF_AT.index(s), parts)

            iteration(-1, 1, 1)
            iteration(0, 0, 1)
            pe.wait_ge(low_summed, 1)
            nc.tensor.matmul(ffn_ps[0][0:1, 0:1], low_sum[:], ones[:], start=True, stop=True).then_inc(low_total, 1)
            pe.wait_ge(flag_ready, 1)
            general = pe.value_load(low_flag[0:1, 0:1].bitcast(I32))
            with pe.If(general > 0):
                main_loop(pe, iteration, 2)
            with pe.Else():
                main_loop(pe, iteration, 1)

        @block.scalar
        def _(act):
            act.wait_ge(const_loaded, 16 * CONST_LOADS)
            nc.scalar.activation(a_neg[:], ch[:, :, C_ALOG:], ACT.Exp).then_inc(const_exp, 1)
            act.wait_ge(const_dve, CONST_DVE)

            def split_slot(k):
                act.wait_ge(raw_loaded[k % 2], 16 * (k // 2 + 1))
                if k >= SPLITS:
                    act.wait_ge(split_stored[k % SPLITS], 32 * (k // SPLITS))
                nc.scalar.activation(split_hi[:, k % SPLITS, :], raw[:, k % 2, :], ACT.Copy).then_inc(split_hi_done, 1)

            def sum_low(k):
                act.wait_ge(split_lo_done, k + 1)
                nc.scalar.activation(raw[:, k % 2, :], split_lo[:, k % SPLITS, :].bitcast(F32), ACT.Abs,
                                     accum_out=low_sums[:, k:k + 1]).then_inc(split_sum_done, 1)

            def load_c(r, n):
                wait_past(act, hC_done, r * TILES + DC * (n - 1))
                act.wait_ge(c_stored, r * 16 + 16)
                act.dma_start(c_rows[:, n % 2], c_dram[r][n].partition_broadcast(P)).then_inc(c_loaded[n % 2], 16)

            def exp_tile(r, par, s):
                n, c = divmod(s, DC)
                if s == 0:
                    act.wait_ge(delta_ready, r * DC + DC)
                wait_past(act, scan_done, r * TILES + (s + 1 - DA_RING))
                nc.scalar.activation(dA[:, s % DA_RING], delta2[:, par, c, :], ACT.Exp, scale=a_neg[:, c, n:n + 1]
                                     ).then_inc(dA_ready, 1)

            def scale_tile(r, par, m):
                n, t = divmod(m, TT)
                if n == 0:
                    act.wait_ge(duT_ready, r * TT + (t + 1))
                if t == 0:
                    wait_past(act, pe_dBu, r * TILES + (n - 1) * DC)
                nc.scalar.activation(dB[:, n % 2, t, :], duT[:, t, :], ACT.Copy, scale=bT2[:, par, t, n:n + 1]
                                     ).then_inc(dB_ready, 1)

            def front_step(r, par, s, end):
                if s in F_XT:
                    k = F_XT.index(s)
                    if k == 0 and end is not None:
                        act.wait_ge(out_stored, end * 16 + 16)
                    act.wait_ge(pe_xT, r * KD + (k + 1))
                    nc.scalar.activation(xT[:, k, :], misc_ps[:], ACT.Copy).then_inc(xT_ready, 1)
                if s - 1 in F_XX:
                    c = F_XX.index(s - 1)
                    act.wait_ge(pe_xx, r * DC + (c + 1))
                    nc.scalar.activation(y2[:, par, c, :], misc_ps[:], ACT.Identity, bias=conv_half[:, c, TAPS:],
                                         scale=conv_half[:, c, TAPS - 1:TAPS]).then_inc(conv_base, 1)
                if s - 2 in F_XX:
                    c = F_XX.index(s - 2)
                    act.wait_ge(conv_taps, r * (DC * (TAPS - 1)) + (c + 1) * (TAPS - 1))
                    nc.scalar.activation(delta2[:, par, c, :], y2[:, par, c, :], ACT.Tanh).then_inc(u_tanh, 1)
                if s == F_DBL_OUT:
                    act.wait_ge(pe_dbl, r + 1)
                    wait_past(act, c_stored, r * 16)
                    nc.scalar.activation(xdbl, misc_ps[0:DTC + STATES, :], ACT.Copy).then_inc(xdbl_ready, 1)
                if s == F_BT_OUT:
                    act.wait_ge(pe_bT, r + 1)
                    nc.scalar.activation(bT2[:, par], misc_ps[:, 0:TT * STATES].rearrange("p (t n) -> p t n", t=TT),
                                         ACT.Copy).then_inc(bT_ready, 1)
                for c in range(DC):
                    if F_EXP[c] != s:
                        continue
                    act.wait_ge(dt_ready, r * DC + (c + 1))
                    nc.scalar.activation(du[:, c, :], delta2[:, par, c, :], ACT.Abs).then_inc(sp_abs, 1)
                    act.wait_ge(sp_abs, r * DC + (c + 1))
                    nc.scalar.activation(du[:, c, :], du[:, c, :], ACT.Exp, scale=-1.0).then_inc(sp_exp, 1)
                if s == F_LN:
                    for c in range(DC):
                        act.wait_ge(sp_lost, r * DC + (c + 1))
                        nc.scalar.activation(sp_w[c], sp_w[c], ACT.Ln).then_inc(sp_ln, 1)
                if s in F_DU:
                    t = F_DU.index(s)
                    act.wait_ge(pe_duT, r * TT + (t + 1))
                    wait_past(act, dB_ready, r * (STATES * TT) + (t + 1 - TT))
                    nc.scalar.activation(duT[:, t, :], misc_ps[:], ACT.Copy).then_inc(duT_ready, 1)

            def tail_xT(r, s, front, end):
                if s in T_XT:
                    k = T_XT.index(s)
                    if front is None and end is not None:
                        act.wait_ge(out_stored, end * 16 + 16)
                    act.wait_ge(pe_tail_xT, r * KD + (k + 1))
                    nc.scalar.activation(xT[:, k, :], misc_ps[:], ACT.Copy).then_inc(tail_xT_ready, 1)

            def tail_step(r, s):
                if s in T_GATE:
                    c = T_GATE.index(s)
                    act.wait_ge(pe_res, r * DC + (c + 1))
                    if c >= 2:
                        act.wait_ge(y_gated, r * DC + (c - 1))
                    nc.scalar.activation(gate[:, c % 2, :], misc_ps[:], ACT.Tanh).then_inc(v_tanh, 1)
                if s in T_X1T:
                    k = T_X1T.index(s)
                    act.wait_ge(pe_x1T, r * KD + (k + 1))
                    nc.scalar.activation(x1T_hi[:, k, :], misc_ps[:], ACT.Copy).then_inc(x1_hi, 1)

            def gelu_tiles(f, tiles):
                for i in tiles:
                    act.wait_ge(pe_half, f * HALVES + 2 * (i + 1))
                    act.wait_ge(ffn_lo, f * FFN_TILES + (HC + i - X32 + 1))
                    nc.scalar.activation(x32[:, i % X32, :], ffn_ps[(2 * HC + i) % 3][:], ACT.Gelu,
                                         scale=fs[:, 2 + i // HC, i % HC:i % HC + 1]).then_inc(gelu_x32, 1)

            def hi_tiles(f, tiles):
                for i in tiles:
                    act.wait_ge(gelu_x32, f * (2 * HC) + (i + 1))
                    if i == HC:
                        act.wait_ge(pe_half, f * HALVES + 2 * HC)
                    dst = hb_hi if i < HC else ha_hi
                    nc.scalar.activation(dst[:, i % HC, :], x32[:, i % X32, :], ACT.Copy).then_inc(ffn_hi, 1)

            def ffn_step(f, s):
                if A_L1 <= s < A_L1 + HC:
                    o = s - A_L1
                    act.wait_ge(pe_l1, f * (2 * HC) + (2 * o + 1))
                    if o >= 2:
                        act.wait_ge(l1_x32, f * HC + (o - 1))
                    nc.scalar.activation(gate[:, o % 2, :], ffn_ps[2 * o % 3][:], ACT.Tanh,
                                         scale=s1_half[:, o:o + 1]).then_inc(l1_tanh, 1)
                if A_L1 + A_HI <= s < A_L1 + A_HI + HC:
                    o = s - A_L1 - A_HI
                    act.wait_ge(l1_x32, f * HC + (o + 1))
                    nc.scalar.activation(ha_hi[:, o, :], x32[:, o % X32, :], ACT.Copy).then_inc(ffn_hi, 1)
                if s in GELU_AT:
                    gelu_tiles(f, GELU_AT[s])
                if s in HI_AT:
                    hi_tiles(f, HI_AT[s])

            def iteration(i, par):
                (scan, spar), (front, fpar), (tail, _), (end, _) = rows(i, par)
                for s in range(TILES):
                    first, count = EXP_AT[s]
                    for step, tile in [(exp_tile, k) for k in range(first, first + count)] + [(scale_tile, s + SCALE_LEAD)]:
                        if tile < TILES:
                            if scan is not None:
                                step(scan, spar, tile)
                        elif front is not None:
                            step(front, fpar, tile - TILES)
                    if (s + 4) % DC == 0:
                        n = (s + 4) // DC
                        if n < STATES:
                            if scan is not None:
                                load_c(scan, n)
                        elif front is not None:
                            load_c(front, 0)
                    if tail is not None:
                        tail_step(tail, s)
                        ffn_step(tail, s)
                    if end is not None:
                        ffn_step(end, s + TILES)
                    if front is not None:
                        front_step(front, fpar, s, end)
                    if scan is not None:
                        tail_xT(scan, s, front, end)
                    if isinstance(i, int) and i == 0:
                        if s in PREP_AT:
                            split_slot(PREP_AT[s])
                        if s - 1 in PREP_AT:
                            sum_low(PREP_AT[s - 1])

            iteration(-1, 1)
            iteration(0, 0)
            main_loop(act, iteration)

        @block.vector
        def _(dve):
            dve.wait_ge(const_loaded, 16 * CONST_LOADS)
            nc.vector.memset(ones[:], 1.0).then_inc(const_dve, 1)
            nc.vector.memset(eps[:], EPS).then_inc(const_dve, 1)
            nc.vector.memset(minus_half[:], -0.5).then_inc(const_dve, 1)
            nc.vector.tensor_scalar(conv_half[:], ch[:, :, 0:TAPS + 1], 0.5, None, ALU.mult).then_inc(const_dve, 1)
            nc.vector.tensor_scalar(inw[:, :, INNER:], inw[:, :, INNER:], 0.5, None, ALU.mult).then_inc(const_dve, 1)
            nc.vector.tensor_scalar(s1_half[:], fs[:, 0, :], 0.5, None, ALU.mult).then_inc(const_dve, 1)
            dve.wait_ge(const_exp, 1)
            nc.vector.tensor_scalar(a_neg[:], a_neg[:], -1.0, None, ALU.mult).then_inc(const_dve, 1)
            dve.wait_ge(const_dve, CONST_DVE)
            nc.vector.tensor_tensor(s12_half[:], s1_half[:], fs[:, 1, :], ALU.mult).then_inc(const_s12, 1)

            def split_low(k):
                dve.wait_ge(split_hi_done, k + 1)
                nc.vector.tensor_tensor(split_lo[:, k % SPLITS, :], raw[:, k % 2, :],
                                        split_hi[:, k % SPLITS, :].bitcast(F32), ALU.subtract
                                        ).then_inc(split_lo_done, 1)

            def scan_tile(r, s):
                dve.wait_ge(dA_ready, r * TILES + (s + 1))
                dve.wait_ge(pe_dBu, r * TILES + (s + 1))
                nc.vector.tensor_tensor_scan(scan_ps[:, s % 4], dA[:, s % DA_RING], scan_ps[:, s % 4], 0.0,
                                             ALU.mult, ALU.add).then_inc(scan_done, 1)

            def c_tile(r, s):
                n, c = divmod(s, DC)
                p = s // 2
                if c == 0:
                    dve.wait_ge(c_loaded[n % 2], r * (16 * STATES // 2) + 16 * (n // 2 + 1))
                if s % 2 == 0:
                    wait_past(dve, y_added, r * PAIRS + (p - 1))
                dve.wait_ge(scan_done, r * TILES + (s + 1))
                nc.vector.tensor_tensor(hC[:, p % 2, s % 2], scan_ps[:, s % 4], c_rows[:, n % 2], ALU.mult
                                        ).then_inc(hC_done, 1)

            def front_step(r, par, s, tail):
                if s - 1 in F_XX:
                    c = F_XX.index(s - 1)
                    for back in range(1, TAPS):
                        if back == 1:
                            dve.wait_ge(conv_base, r * DC + (c + 1))
                        else:
                            dve.wait_ge(conv_taps, r * (DC * (TAPS - 1)) + (c * (TAPS - 1) + back - 1))
                        tap = TAPS - 1 - back
                        nc.vector.scalar_tensor_tensor(
                            out=y2[:, par, c, back:], in0=misc_ps[:, 0:SEQ - back], scalar=conv_half[:, c, tap:tap + 1],
                            in1=y2[:, par, c, back:], op0=ALU.mult, op1=ALU.add).then_inc(conv_taps, 1)
                if s - 2 in F_XX:
                    c = F_XX.index(s - 2)
                    dve.wait_ge(u_tanh, r * DC + (c + 1))
                    nc.vector.scalar_tensor_tensor(out=y2[:, par, c, :], in0=delta2[:, par, c, :], scalar=1.0,
                                                   in1=y2[:, par, c, :], op0=ALU.add, op1=ALU.mult
                                                   ).then_inc(u_ready, 1)
                if s - 1 in F_DT:
                    c = F_DT.index(s - 1)
                    dve.wait_ge(pe_dt, r * DC + (c + 1))
                    nc.vector.tensor_scalar(delta2[:, par, c, :], misc_ps[:], ch[:, c, C_DTB:C_DTB + 1], None,
                                            ALU.add).then_inc(dt_ready, 1)
                for c in range(DC):
                    if F_PLUS[c] != s:
                        continue
                    if c == 3:
                        dve.wait_ge(c_stored, r * 16 + 16)
                        dve.wait_ge(pe_bT, r + 1)
                    if c == 1 and tail is not None:
                        dve.wait_ge(l1_x32, tail * HC + HC)
                    dve.wait_ge(sp_exp, r * DC + (c + 1))
                    nc.vector.tensor_scalar(sp_w[c], du[:, c, :], 1.0, None, ALU.add).then_inc(sp_plus, 1)
                    dve.wait_ge(sp_plus, r * DC + (c + 1))
                    nc.vector.scalar_tensor_tensor(out=du[:, c, :], in0=sp_w[c], scalar=1.0, in1=du[:, c, :],
                                                   op0=ALU.subtract, op1=ALU.subtract).then_inc(sp_lost, 1)
                for c in range(DC):
                    if F_MAX[c] != s:
                        continue
                    dve.wait_ge(sp_lost, r * DC + (c + 1))
                    nc.vector.scalar_tensor_tensor(out=delta2[:, par, c, :], in0=delta2[:, par, c, :], scalar=0.0,
                                                   in1=du[:, c, :], op0=ALU.max, op1=ALU.subtract).then_inc(sp_max, 1)
                for c in range(DC):
                    if F_DELTA[c] == s:
                        dve.wait_ge(sp_max, r * DC + (c + 1))
                        dve.wait_ge(sp_ln, r * DC + (c + 1))
                        nc.vector.tensor_tensor(delta2[:, par, c, :], delta2[:, par, c, :], sp_w[c], ALU.add
                                                ).then_inc(delta_ready, 1)
                for c in range(DC):
                    if F_DELTA_U[c] == s:
                        dve.wait_ge(delta_ready, r * DC + (c + 1))
                        nc.vector.tensor_tensor(du[:, c, :], y2[:, par, c, :], delta2[:, par, c, :], ALU.mult
                                                ).then_inc(du_ready, 1)
                for c in range(DC):
                    if F_Y[c] != s:
                        continue
                    dve.wait_ge(du_ready, r * DC + (c + 1))
                    nc.vector.tensor_scalar(y2[:, par, c, :], y2[:, par, c, :], ch[:, c, C_D:C_D + 1], None,
                                            ALU.mult).then_inc(y_init, 1)

            def statistics(which, src, r, half, ready):
                dve.wait_ge(ready, r * 2 + (half + 1))
                for t in (2 * half, 2 * half + 1):
                    nc.vector.bn_stats(stats[:, which, t, :], src[:, t, :]).then_inc(ln_stats[which], 1)
                if half:
                    dve.wait_ge(ln_stats[which], r * TT + TT)
                    nc.vector.tensor_copy(stats_seen[:, which:which + 1], stats[:, which, TT - 1, 0:1])
                    for t in range(TT):
                        nc.vector.bn_aggr(mv[:, which, t, :], stats[:, which, t, :]).then_inc(ln_aggr[which], 1)

            def normalise(which, src, dst, r, done):
                dve.wait_ge(ln_rstd[which], r + 1)
                for t in range(TT):
                    nc.vector.tensor_scalar(dst[:, t, :], src[:, t, :], mv[:, which, t, 0:1],
                                            rstd[:, which, t:t + 1], ALU.subtract, ALU.mult).then_inc(done, 1)

            def tail_step(r, par, s):
                if s in T_GATE:
                    c = T_GATE.index(s)
                    dve.wait_ge(v_tanh, r * DC + (c + 1))
                    nc.vector.scalar_tensor_tensor(out=gate[:, c % 2, :], in0=gate[:, c % 2, :], scalar=1.0,
                                                   in1=misc_ps[:], op0=ALU.add, op1=ALU.mult).then_inc(v_ready, 1)
                if s in T_ADD:
                    k = T_ADD.index(s)
                    dve.wait_ge(pe_out, r * TT + (2 * k + 2))
                    nc.vector.tensor_tensor(xt[:, 2 * k:2 * k + 2, :], out_ps[k][:].rearrange("p (t d) -> p t d", t=2),
                                            xt[:, 2 * k:2 * k + 2, :], ALU.add).then_inc(z_ready, 1)
                if s in T_STATS:
                    statistics(0, xt, r, T_STATS.index(s), z_ready)
                if s == T_NORM:
                    normalise(0, xt, x1, r, x1_ready)
                if s in T_X1T:
                    k = T_X1T.index(s)
                    dve.wait_ge(x1_hi, r * KD + (k + 1))
                    nc.vector.tensor_tensor(x1T_lo[:, k, :], misc_ps[:], x1T_hi[:, k, :].bitcast(F32), ALU.subtract
                                            ).then_inc(x1_lo, 1)

            def l1_tile(f, o):
                dve.wait_ge(l1_tanh, f * HC + (o + 1))
                nc.vector.scalar_tensor_tensor(out=gate[:, o % 2, :], in0=gate[:, o % 2, :], scalar=1.0,
                                               in1=ffn_ps[2 * o % 3][:], op0=ALU.add, op1=ALU.mult
                                               ).then_inc(l1_gate, 1)
                dve.wait_ge(l1_gate, f * HC + (o + 1))
                dve.wait_ge(pe_l1, f * (2 * HC) + (2 * o + 2))
                if o >= X32:
                    dve.wait_ge(ffn_lo, f * FFN_TILES + (o - X32 + 1))
                nc.vector.scalar_tensor_tensor(out=x32[:, o % X32, :], in0=gate[:, o % 2, :],
                                               scalar=s12_half[:, o:o + 1], in1=ffn_ps[(2 * o + 1) % 3][:],
                                               op0=ALU.mult, op1=ALU.mult).then_inc(l1_x32, 1)

            def end_step(f, s):
                if s in E_SCALE:
                    k = E_SCALE.index(s)
                    dve.wait_ge(pe_w3, f * TT + 2 * (k + 1))
                    nc.vector.tensor_tensor(out_st[:, 2 * k:2 * k + 2, :],
                                            ffn_ps[(4 * HC + k) % 3][:].rearrange("p (t d) -> p t d", t=2),
                                            w3s[:].unsqueeze(1).to_broadcast([P, 2, DIM]), ALU.mult
                                            ).then_inc(w3_scaled, 1)
                if s in E_ADD:
                    k = E_ADD.index(s)
                    dve.wait_ge(w3_scaled, f * 2 + (k + 1))
                    nc.vector.tensor_tensor(out_st[:, 2 * k:2 * k + 2, :], out_st[:, 2 * k:2 * k + 2, :],
                                            x1[:, 2 * k:2 * k + 2, :], ALU.add).then_inc(z2_ready, 1)
                if s in E_STATS:
                    statistics(1, out_st, f, E_STATS.index(s), z2_ready)
                if s == E_NORM:
                    normalise(1, out_st, out_st, f, out_ready)

            def iteration(i, par):
                (scan, _), (front, fpar), (tail, tpar), (end, _) = rows(i, par)
                for s in range(TILES):
                    if scan is not None:
                        scan_tile(scan, s)
                        c_tile(scan, s)
                    if end is not None:
                        end_step(end, s)
                    if tail is not None:
                        tail_step(tail, tpar, s)
                    if front is not None:
                        front_step(front, fpar, s, tail)
                    if tail is not None and A_L1 <= s < A_L1 + HC:
                        l1_tile(tail, s - A_L1)
                    if isinstance(i, int) and i == 0 and s in PREP_AT:
                        split_low(PREP_AT[s])

            iteration(-1, 1)
            iteration(0, 0)
            dve.wait_ge(split_sum_done, SLOTS)
            nc.vector.tensor_reduce(low_sum[:], low_sums[:], mybir.AxisListType.X, ALU.add).then_inc(low_summed, 1)
            dve.wait_ge(low_total, 1)
            nc.vector.tensor_copy(low_flag[:], ffn_ps[0][0:1, 0:1]).then_inc(flag_ready, 1)
            main_loop(dve, iteration)

        @block.gpsimd
        def _(pool):
            pool.wait_ge(const_dve, CONST_DVE)

            def y_pair(r, par, p):
                pool.wait_ge(hC_done, r * TILES + (2 * p + 2))
                if p == 0:
                    pool.wait_ge(y_init, r * DC + DC)
                if p >= 2:
                    pool.wait_ge(y_added, r * PAIRS + (p - 1))
                c = 2 * (p % 2)
                nc.gpsimd.tensor_tensor(y2[:, par, c:c + 2, :], y2[:, par, c:c + 2, :], hC[:, p % 2], ALU.add
                                        ).then_inc(y_added, 1)

            def gate_tile(r, par, c):
                if c == 0:
                    pool.wait_ge(y_added, r * PAIRS + PAIRS)
                pool.wait_ge(v_ready, r * DC + (c + 1))
                nc.gpsimd.tensor_tensor(y2[:, par, c, :], y2[:, par, c, :], gate[:, c % 2, :], ALU.mult
                                        ).then_inc(y_gated, 1)

            def rstd_of(which, r):
                pool.wait_ge(ln_aggr[which], r * TT + TT)
                nc.gpsimd.tensor_tensor(var_eps[:, which], mv[:, which, :, 1], eps[:], ALU.add
                                        ).then_inc(ln_eps[which], 1)
                pool.wait_ge(ln_eps[which], r + 1)
                nc.gpsimd.tensor_tensor(rstd[:, which], var_eps[:, which], minus_half[:], ALU.pow
                                        ).then_inc(ln_rstd[which], 1)

            def low_tile(f, i):
                pool.wait_ge(ffn_hi, f * FFN_TILES + (i + 1))
                hi, lo = (hb_hi, hb_lo) if HC <= i < 2 * HC else (ha_hi, ha_lo)
                nc.gpsimd.tensor_tensor(lo[:, i % HC, :], x32[:, i % X32, :], hi[:, i % HC, :].bitcast(F32),
                                        ALU.subtract).then_inc(ffn_lo, 1)

            def ffn_step(f, s):
                if A_L1 + A_LO <= s < A_L1 + A_LO + HC:
                    low_tile(f, s - A_L1 - A_LO)
                for i in HI_AT.get(s - LO_AFTER, ()):
                    low_tile(f, HC + i)

            def iteration(i, par):
                (scan, spar), (front, fpar), (tail, tpar), (end, _) = rows(i, par)
                for s in range(TILES):
                    if scan is not None and s % 2:
                        y_pair(scan, spar, s // 2)
                    if tail is not None:
                        if s - 1 in T_GATE:
                            gate_tile(tail, tpar, T_GATE.index(s - 1))
                        if s == T_STATS[-1]:
                            rstd_of(0, tail)
                        ffn_step(tail, s)
                    if end is not None:
                        if s == E_STATS[-1]:
                            rstd_of(1, end)
                        ffn_step(end, s + TILES)

            iteration(-1, 1)
            iteration(0, 0)
            main_loop(pool, iteration)


def kernel(L0_attn_x, L0_attn_in_w, L0_attn_conv_w, L0_attn_conv_b, L0_attn_xproj_w, L0_attn_dt_w, L0_attn_dt_b,
           L0_attn_A_log, L0_attn_D, L0_attn_out_w, L0_ffn_w1_w, L0_ffn_w1_s, L0_ffn_w2_w, L0_ffn_w2_s,
           L0_ffn_h1_w, L0_ffn_h1_s, L0_ffn_h2_w, L0_ffn_h2_s, L0_ffn_w3_w, L0_ffn_w3_s):
    import numpy as np
    import concourse.bacc as bacc
    from concourse.bass_utils import run_bass_kernel_spmd

    def ktiles(wT):
        return wT.reshape(-1, P, wT.shape[1]).transpose(1, 0, 2)

    def channels(a):
        return a.reshape(-1, P, a.shape[1]).transpose(1, 0, 2)

    A = np.asarray
    chan = np.concatenate([channels(A(L0_attn_conv_w)[:, 0, :])]
                          + [channels(A(a)[:, None]) for a in (L0_attn_conv_b, L0_attn_D, L0_attn_dt_b)]
                          + [channels(A(L0_attn_A_log))], axis=2)
    w1, w2, h1, h2, w3 = (ktiles(A(w).T) for w in (L0_ffn_w1_w, L0_ffn_w2_w, L0_ffn_h1_w, L0_ffn_h2_w, L0_ffn_w3_w))
    slots = []
    for s in range(L1_SLOTS):
        tiles = [w[:, :, o * P:(o + 1) * P] for o in (2 * s, 2 * s + 1) for w in (w1, w2)]
        slots.append(np.concatenate(tiles, axis=1).reshape(P, SLOT_COLS))
    for w in (h1, h2):
        slots += [w[:, :, o * P:(o + 1) * P].reshape(P, SLOT_COLS) for o in range(HC)]
    slots += [w3[:, 4 * h:4 * h + 4, :].reshape(P, SLOT_COLS) for h in range(W3_SLOTS)]
    scales = np.concatenate([channels(A(s)[:, None]).transpose(0, 2, 1)
                             for s in (L0_ffn_w1_s, L0_ffn_w2_s, L0_ffn_h1_s, L0_ffn_h2_s)], axis=1)
    arrays = {
        "x_tok": A(L0_attn_x).reshape(BATCH, TT, P, DIM).transpose(0, 2, 1, 3),
        "in_wT": ktiles(A(L0_attn_in_w).T),
        "chan": chan,
        "xproj_wT": ktiles(A(L0_attn_xproj_w).T)[:, :, np.r_[0:RANK, RANK + STATES:RANK + 2 * STATES,
                                                             RANK:RANK + STATES]],
        "dt_wT": A(L0_attn_dt_w).T,
        "out_wT": ktiles(A(L0_attn_out_w).T),
        "ffn_w": np.stack(slots),
        "ffn_s": scales,
        "w3_s": A(L0_ffn_w3_s),
        "identity": np.eye(P, dtype=np.float32),
    }
    arrays = {n: np.ascontiguousarray(a) for n, a in arrays.items()}
    nc = bacc.Bacc("TRN2", target_bir_lowering=False, num_devices=1)
    args = [nc.dram_tensor(n, list(a.shape), mybir.dt.from_np(a.dtype), kind="ExternalInput").ap()
            for n, a in arrays.items()]
    out = nc.dram_tensor("out_tok", [BATCH, P, TT, DIM], F32, kind="ExternalOutput").ap()
    build(nc, *args, out)
    r = run_bass_kernel_spmd(nc, [arrays], core_ids=[0])
    return r.results[0]["out_tok"].transpose(0, 2, 1, 3).reshape(BATCH, SEQ, DIM)
```
